# Optimizing a Trainium2 kernel written in Bass

```python
import numpy as np
import jax
import jax.numpy as jnp

def _softmax(x, axis=-1):
    return jax.nn.softmax(x, axis=axis)

def _gelu(x):
    return jax.nn.gelu(x, approximate=True)

def _silu(x):
    return jax.nn.silu(x)

def _sigmoid(x):
    return jax.nn.sigmoid(x)

def _layernorm(x, axis=-1, eps=1e-05):
    m = jnp.mean(x, axis=axis, keepdims=True)
    v = jnp.var(x, axis=axis, keepdims=True)
    return (x - m) / jnp.sqrt(v + eps)

def _scatter_add(tgt, idx, src, axis=0):
    return tgt.at[idx].add(src)

def _segment_sum(src, seg, n):
    return jax.ops.segment_sum(src, seg, n)
kernel_name = 'mk_rec_standalone_d1_rec_r8_d6fe87'

def setup_inputs(seed: int=0):
    np.random.seed(seed)
    _w = jnp.asarray

    def _rec_inputs():
        import jax
        import jax.numpy as jnp
        _rk = jax.random.key(seed)
        r_dense_inputs = -0.00608245 + 1.00131 * jax.random.normal(jax.random.fold_in(_rk, 1), (2048, 8), jnp.float32)
        r_sparse_inputs = jnp.stack([jax.random.randint(jax.random.fold_in(jax.random.fold_in(_rk, 2), 0), (2048,), 20, 99981, jnp.int32), jax.random.randint(jax.random.fold_in(jax.random.fold_in(_rk, 2), 1), (2048,), 8, 12498, jnp.int32), jax.random.randint(jax.random.fold_in(jax.random.fold_in(_rk, 2), 2), (2048,), 23, 99994, jnp.int32)], axis=1)
        r_seq_inputs = jax.random.randint(jax.random.fold_in(_rk, 3), (2048, 40, 2), 0, 12500, jnp.int32)
        r_item_inputs = jnp.stack([jax.random.randint(jax.random.fold_in(jax.random.fold_in(_rk, 4), 0), (2048,), 9, 99996, jnp.int32), jax.random.randint(jax.random.fold_in(jax.random.fold_in(_rk, 4), 1), (2048,), 15, 99995, jnp.int32)], axis=1)
        return (r_dense_inputs, r_sparse_inputs, r_seq_inputs, r_item_inputs)
    r_dense_inputs, r_sparse_inputs, r_seq_inputs, r_item_inputs = _rec_inputs()

    def _L0_rec_setup():
        import jax, jax.numpy as jnp
        import numpy as np
        B, L, NB = (1024, 40, 2)
        V, E = (12500, 64)
        NS, ND = (3, 8)
        D = NB * E
        ALL = D + D + (ND + NS * E)
        NEG_INF = -2.0 ** 32 + 1
        BN_EPS = 0.001

        def prelu(x, alpha):
            return jnp.where(x > 0, x, alpha * x)
        key = jax.random.key(seed)
        ks = jax.random.split(key, 20)
        inp = {'dense_inputs': jax.random.normal(ks[0], (B, ND), jnp.float32), 'sparse_inputs': jax.random.randint(ks[1], (B, NS), 0, V), 'seq_inputs': jax.random.randint(ks[2], (B, L, NB), 0, V), 'item_inputs': jax.random.randint(ks[3], (B, NB), 0, V), 'emb_sparse': jax.random.uniform(ks[4], (NS, V, E), jnp.float32, -0.05, 0.05), 'emb_seq': jax.random.uniform(ks[5], (NB, V, E), jnp.float32, -0.05, 0.05), 'att_W1': jax.random.normal(ks[6], (4 * D, 80), jnp.float32) * 0.05, 'att_b1': jnp.zeros((80,), jnp.float32), 'att_W2': jax.random.normal(ks[7], (80, 40), jnp.float32) * 0.05, 'att_b2': jnp.zeros((40,), jnp.float32), 'att_Wf': jax.random.normal(ks[8], (40, 1), jnp.float32) * 0.05, 'att_bf': jnp.zeros((1,), jnp.float32), 'bn_gamma': jnp.ones((ALL,), jnp.float32), 'bn_beta': jnp.zeros((ALL,), jnp.float32), 'bn_mean': jnp.zeros((ALL,), jnp.float32), 'bn_var': jnp.ones((ALL,), jnp.float32), 'ffn_W1': jax.random.normal(ks[9], (ALL, 80), jnp.float32) * 0.05, 'ffn_b1': jnp.zeros((80,), jnp.float32), 'ffn_a1': jnp.full((80,), 0.25, jnp.float32), 'ffn_W2': jax.random.normal(ks[10], (80, 40), jnp.float32) * 0.05, 'ffn_b2': jnp.zeros((40,), jnp.float32), 'ffn_a2': jnp.full((40,), 0.25, jnp.float32), 'out_W': jax.random.normal(ks[11], (40, 1), jnp.float32) * 0.05, 'out_b': jnp.zeros((1,), jnp.float32)}
        return inp
    _L0_rec_all = _L0_rec_setup()
    _L0_rec_in = {k: v for k, v in _L0_rec_all.items() if k in ('emb_sparse', 'emb_seq', 'att_W1', 'att_b1', 'att_W2', 'att_b2', 'att_Wf', 'att_bf', 'bn_gamma', 'bn_beta', 'bn_mean', 'bn_var', 'ffn_W1', 'ffn_b1', 'ffn_a1', 'ffn_W2', 'ffn_b2', 'ffn_a2', 'out_W', 'out_b')}
    del _L0_rec_all
    return {'r_dense_inputs': r_dense_inputs, 'r_sparse_inputs': r_sparse_inputs, 'r_seq_inputs': r_seq_inputs, 'r_item_inputs': r_item_inputs, 'L0_rec_emb_sparse': _L0_rec_in['emb_sparse'], 'L0_rec_emb_seq': _L0_rec_in['emb_seq'], 'L0_rec_att_W1': _L0_rec_in['att_W1'], 'L0_rec_att_b1': _L0_rec_in['att_b1'], 'L0_rec_att_W2': _L0_rec_in['att_W2'], 'L0_rec_att_b2': _L0_rec_in['att_b2'], 'L0_rec_att_Wf': _L0_rec_in['att_Wf'], 'L0_rec_att_bf': _L0_rec_in['att_bf'], 'L0_rec_bn_gamma': _L0_rec_in['bn_gamma'], 'L0_rec_bn_beta': _L0_rec_in['bn_beta'], 'L0_rec_bn_mean': _L0_rec_in['bn_mean'], 'L0_rec_bn_var': _L0_rec_in['bn_var'], 'L0_rec_ffn_W1': _L0_rec_in['ffn_W1'], 'L0_rec_ffn_b1': _L0_rec_in['ffn_b1'], 'L0_rec_ffn_a1': _L0_rec_in['ffn_a1'], 'L0_rec_ffn_W2': _L0_rec_in['ffn_W2'], 'L0_rec_ffn_b2': _L0_rec_in['ffn_b2'], 'L0_rec_ffn_a2': _L0_rec_in['ffn_a2'], 'L0_rec_out_W': _L0_rec_in['out_W'], 'L0_rec_out_b': _L0_rec_in['out_b']}

def reference(r_dense_inputs, r_sparse_inputs, r_seq_inputs, r_item_inputs, L0_rec_emb_sparse, L0_rec_emb_seq, L0_rec_att_W1, L0_rec_att_b1, L0_rec_att_W2, L0_rec_att_b2, L0_rec_att_Wf, L0_rec_att_bf, L0_rec_bn_gamma, L0_rec_bn_beta, L0_rec_bn_mean, L0_rec_bn_var, L0_rec_ffn_W1, L0_rec_ffn_b1, L0_rec_ffn_a1, L0_rec_ffn_W2, L0_rec_ffn_b2, L0_rec_ffn_a2, L0_rec_out_W, L0_rec_out_b):
    import jax
    import jax.numpy as jnp

    def _L0_rec_ref(dense_inputs, sparse_inputs, seq_inputs, item_inputs, emb_sparse, emb_seq, att_W1, att_b1, att_W2, att_b2, att_Wf, att_bf, bn_gamma, bn_beta, bn_mean, bn_var, ffn_W1, ffn_b1, ffn_a1, ffn_W2, ffn_b2, ffn_a2, out_W, out_b):
        import jax, jax.numpy as jnp
        import numpy as np
        B, L, NB = (1024, 40, 2)
        V, E = (12500, 64)
        NS, ND = (3, 8)
        D = NB * E
        ALL = D + D + (ND + NS * E)
        NEG_INF = -2.0 ** 32 + 1
        BN_EPS = 0.001

        def prelu(x, alpha):
            return jnp.where(x > 0, x, alpha * x)
        mask = seq_inputs[:, :, 0] != 0
        other_info = jnp.concatenate([dense_inputs] + [emb_sparse[i][sparse_inputs[:, i]] for i in range(NS)], axis=-1)
        seq_embed = jnp.concatenate([emb_seq[i][seq_inputs[:, :, i]] for i in range(NB)], axis=-1)
        item_embed = jnp.concatenate([emb_seq[i][item_inputs[:, i]] for i in range(NB)], axis=-1)
        q = jnp.broadcast_to(item_embed[:, None, :], seq_embed.shape)
        info = jnp.concatenate([q, seq_embed, q - seq_embed, q * seq_embed], axis=-1)
        h = jax.nn.sigmoid(info @ att_W1 + att_b1)
        h = jax.nn.sigmoid(h @ att_W2 + att_b2)
        logits = (h @ att_Wf + att_bf)[..., 0]
        logits = jnp.where(mask, logits, NEG_INF)
        att = jax.nn.softmax(logits, axis=-1)
        user_info = jnp.einsum('bl,bld->bd', att, seq_embed)
        info_all = jnp.concatenate([user_info, item_embed, other_info], axis=-1)
        info_all = bn_gamma * (info_all - bn_mean) * jax.lax.rsqrt(bn_var + BN_EPS) + bn_beta
        info_all = prelu(info_all @ ffn_W1 + ffn_b1, ffn_a1)
        info_all = prelu(info_all @ ffn_W2 + ffn_b2, ffn_a2)
        return jax.nn.sigmoid(info_all @ out_W + out_b)
    y = _L0_rec_ref(r_dense_inputs, r_sparse_inputs, r_seq_inputs, r_item_inputs, L0_rec_emb_sparse, L0_rec_emb_seq, L0_rec_att_W1, L0_rec_att_b1, L0_rec_att_W2, L0_rec_att_b2, L0_rec_att_Wf, L0_rec_att_bf, L0_rec_bn_gamma, L0_rec_bn_beta, L0_rec_bn_mean, L0_rec_bn_var, L0_rec_ffn_W1, L0_rec_ffn_b1, L0_rec_ffn_a1, L0_rec_ffn_W2, L0_rec_ffn_b2, L0_rec_ffn_a2, L0_rec_out_W, L0_rec_out_b)
    return y

_drawn_inputs = setup_inputs


def setup_inputs(seed=0):
    import zlib

    import numpy as np

    out = dict(_drawn_inputs(seed))
    spreads = {'L0_rec_att_b1': (0.0, 2.0),
     'L0_rec_att_b2': (0.0, 2.0),
     'L0_rec_bn_gamma': (1.0, 0.6),
     'L0_rec_bn_beta': (0.0, 0.8),
     'L0_rec_bn_mean': (0.0, 0.8),
     'L0_rec_bn_var': (1.0, 0.6),
     'L0_rec_ffn_b1': (0.0, 2.0),
     'L0_rec_ffn_a1': (0.25, 0.6),
     'L0_rec_ffn_b2': (0.0, 2.0),
     'L0_rec_ffn_a2': (0.25, 0.6)}
    factors = {'r_dense_inputs': 8.0,
     'L0_rec_emb_sparse': 8.0,
     'L0_rec_emb_seq': 8.0,
     'L0_rec_att_W1': 64.0,
     'L0_rec_att_W2': 64.0,
     'L0_rec_att_Wf': 64.0,
     'L0_rec_ffn_W1': 8.0,
     'L0_rec_ffn_W2': 6.857}
    for name, (base, spread) in spreads.items():
        noise = np.random.default_rng([zlib.crc32(name.encode()), seed]).standard_normal(out[name].shape)
        drawn = base * np.exp(spread * noise) if base else spread * noise
        out[name] = jnp.asarray(drawn.astype(out[name].dtype))
    for name, factor in factors.items():
        out[name] = (out[name] * factor).astype(out[name].dtype)
    return out
```

```python
from contextlib import ExitStack

import concourse.bass as bass
from concourse import mybir

F32 = mybir.dt.float32
I32 = mybir.dt.int32
ALU = mybir.AluOpType
ACT = mybir.ActivationFunctionType
AX = mybir.AxisListType

P = 128
MASKED = -2.0 ** 32 + 1
BN_EPS = 0.001


def build(nc, dense, sparse, seq, item, emb_sparse, emb_seq, att_w1, att_b1, att_w2, att_b2, att_wf, att_bf,
          bn_gamma, bn_beta, bn_mean, bn_var, ffn_w1, ffn_b1, ffn_a1, ffn_w2, ffn_b2, ffn_a2, out_w, out_b, out):
    ROWS, L, NB = seq.shape
    V, E = emb_seq.shape[1:]
    NS, ND = sparse.shape[1], dense.shape[1]
    D = NB * E
    A1, A2 = att_w2.shape
    H1, H2 = ffn_w2.shape
    TILES = ROWS // P
    PAIRS = TILES // 2
    G = 4
    GROUPS = L // G
    N = G * P
    SEQ, NI = L * NB, L * NB + NB
    NX = NI + NS
    UP = 64
    assert D == P and A2 <= UP and GROUPS == 10 and TILES % 2 == 0

    seq_table = emb_seq.rearrange("n v e -> (n v) e")
    sparse_table = emb_sparse.rearrange("n v e -> (n v) e")
    USER, ITEM, DENSE = (0, D), (D, D), (2 * D, ND)
    SPARSE_A, SPARSE_B = (2 * D + ND, 2 * E), (2 * D + ND + 2 * E, (NS - 2) * E)
    CHUNKS = [USER, ITEM, DENSE, SPARSE_A, SPARSE_B]

    ctx = ExitStack()
    with ctx:
        def sb(name, shape, dt=F32):
            return ctx.enter_context(nc.sbuf_tensor(name, shape, dt))

        def ps(name):
            return ctx.enter_context(nc.psum_tensor(name, [P, 512], F32))

        def sem(name):
            return ctx.enter_context(nc.semaphore(name))

        raw = sb("raw", [P, TILES + 1, NX], I32)
        wrap = sb("wrap", [P, NX])
        table_start = sb("table_start", [P, NX])
        idx = [sb(f"idx{h}", [P, NX], I32) for h in range(2)]
        masked = [sb(f"masked{h}", [P, L], I32) for h in range(2)]
        masked_logit = sb("masked_logit", [P, L])
        hist = sb("hist", [P, 2, L * D])
        items = sb("items", [P, 2, D])
        sparse_rows = sb("sparse_rows", [P, 2, NS * E])
        dense_rows = sb("dense_rows", [P, TILES, ND])
        dense_now = sb("dense_now", [P, ND])
        ident = sb("ident", [P, P])
        w1_raw = sb("w1_raw", [P, 4, A1])
        w1_item = sb("w1_item", [P, A1])
        w1_hist = sb("w1_hist", [P, A1])
        w1_prod = w1_raw[:, 3, :]
        b1 = sb("b1", [A1, 1])
        w2 = sb("w2", [A1, UP])
        b2 = sb("b2", [P, 1])
        wf = sb("wf", [P, 2])
        bf = sb("bf", [P, 1])
        fw1 = sb("fw1", [P, len(CHUNKS), H1])
        fb1 = sb("fb1", [H1, 1])
        fa1 = sb("fa1", [H1, 1])
        fw2 = sb("fw2", [H1, H2])
        fb2 = sb("fb2", [H2, 1])
        fa2 = sb("fa2", [H2, 1])
        ow = sb("ow", [H2, 1])
        ob = sb("ob", [1, 1])
        bn = sb("bn", [P, 4, len(CHUNKS)])
        bn_x = sb("bn_x", [P, 3, len(CHUNKS)])
        std = sb("std", [P, len(CHUNKS)])
        eps = sb("eps", [P, 1])
        bn_scale = sb("bn_scale", [P, len(CHUNKS)])
        bn_shift = sb("bn_shift", [P, len(CHUNKS)])
        hist_t = sb("hist_t", [P, 2, N])
        prod_t = sb("prod_t", [P, 2, N])
        hidden1 = sb("hidden1", [A1, 2, N])
        hidden2 = sb("hidden2", [P, N // 2])
        item_t = sb("item_t", [P, P])
        item_part = sb("item_part", [A1, P])
        logit = sb("logit", [P, L])
        neg_max = sb("neg_max", [P, 1])
        weight = sb("weight", [P, L])
        total = sb("total", [P, 1])
        inv_total = sb("inv_total", [P, 1])
        odd_sum = sb("odd_sum", [P, D])
        user = sb("user", [P, D])
        x = sb("x", [P, len(CHUNKS), P])
        z1 = sb("z1", [H1, P])
        n1 = sb("n1", [H1, P])
        y1 = sb("y1", [H1, P])
        z2 = sb("z2", [H2, P])
        n2 = sb("n2", [H2, P])
        y2 = sb("y2", [H2, P])
        score = sb("score", [1, ROWS])

        turned = [ps(f"turned{s}") for s in range(2)]
        pre1 = [ps(f"pre1{s}") for s in range(2)]
        pre2 = ps("pre2")
        logits = ps("logits")
        small = ps("small")
        sums = ps("sums")
        even_acc, odd_acc = sums[:, 0:D], sums[:, D:2 * D]

        idx_loaded = sem("idx_loaded")
        idx_rest_loaded = sem("idx_rest_loaded")
        att_weights_loaded = sem("att_weights_loaded")
        ffn_weights_loaded = sem("ffn_weights_loaded")
        stored = sem("stored")
        padded = sem("padded")
        dense_ready = sem("dense_ready")
        ident_zeroed = sem("ident_zeroed")
        ident_ready = sem("ident_ready")
        w1_ready = sem("w1_ready")
        bn_step = sem("bn_step")
        bn_ready = sem("bn_ready")
        std_ready = sem("std_ready")
        idx_ready = sem("idx_ready")
        idx_step = sem("idx_step")
        items_landed = [sem(f"items_landed{h}") for h in range(2)]
        sparse_landed = [sem(f"sparse_landed{h}") for h in range(2)]
        group_landed = [sem(f"group_landed{s}") for s in range(2)]
        group_ready = sem("group_ready")
        tile_consumed = sem("tile_consumed")
        group_turned = sem("group_turned")
        group_copied = sem("group_copied")
        product_ready = sem("product_ready")
        layer1_done = sem("layer1_done")
        item_added = sem("item_added")
        hidden1_ready = sem("hidden1_ready")
        layer2_done = sem("layer2_done")
        hidden2_ready = sem("hidden2_ready")
        item_turned = sem("item_turned")
        item_copied = sem("item_copied")
        item_part_done = sem("item_part_done")
        item_part_ready = sem("item_part_ready")
        logits_done = sem("logits_done")
        softmax_step = sem("softmax_step")
        max_ready = sem("max_ready")
        weights_ready = sem("weights_ready")
        sum_step = sem("sum_step")
        user_step = sem("user_step")
        user_ready = sem("user_ready")
        side_turned = sem("side_turned")
        side_copied = sem("side_copied")
        user_turned = sem("user_turned")
        user_copied = sem("user_copied")
        ffn1_done = sem("ffn1_done")
        z1_ready = sem("z1_ready")
        n1_ready = sem("n1_ready")
        y1_ready = sem("y1_ready")
        ffn2_done = sem("ffn2_done")
        z2_ready = sem("z2_ready")
        n2_ready = sem("n2_ready")
        y2_ready = sem("y2_ready")
        score_done = sem("score_done")
        score_ready = sem("score_ready")

        def wait(eng, semaphore, count):
            eng.wait_ge(semaphore, count)
            eng.nop(nofuse=True)

        block = ctx.enter_context(nc.Block())

        @block.sync
        def _(sp):
            seq_t = seq.rearrange("(t p) l n -> p t (l n)", p=P)
            item_tiles = item.rearrange("(t p) n -> p t n", p=P)
            sparse_tiles = sparse.rearrange("(t p) n -> p t n", p=P)
            with nc.allow_non_contiguous_dma(reason="short index rows and vectors by partition"):
                sp.dma_start(raw[:, 0, 0:SEQ], seq_t[:, 0, :]).then_inc(idx_loaded, 16)
                sp.dma_start(raw[:, 0, SEQ:NI], item_tiles[:, 0, :]).then_inc(idx_loaded, 16)
                sp.dma_start(raw[:, 0, NI:NX], sparse_tiles[:, 0, :]).then_inc(idx_loaded, 16)
                sp.dma_start(w1_raw[:, :, :], att_w1.rearrange("(c p) n -> p c n", p=P)).then_inc(att_weights_loaded, 16)
                sp.dma_start(b1[:, :], att_b1.rearrange("(p o) -> p o", o=1)).then_inc(att_weights_loaded, 16)
                sp.wait_ge(padded, 1)
                sp.dma_start(w2[:, 0:A2], att_w2).then_inc(att_weights_loaded, 16)
                for half in range(2):
                    rows = slice(UP * half, UP * half + A2)
                    sp.dma_start(b2[rows, :], att_b2.rearrange("(p o) -> p o", o=1)).then_inc(att_weights_loaded, 16)
                    sp.dma_start(wf[rows, half:half + 1], att_wf).then_inc(att_weights_loaded, 16)
                sp.dma_start(bf[:, :], att_bf.rearrange("(p o) -> p o", o=1).broadcast_to([P, 1]))\
                    .then_inc(att_weights_loaded, 16)
                sp.dma_start(raw[:, 1:TILES, 0:SEQ], seq_t[:, 1:TILES, :]).then_inc(idx_rest_loaded, 16)
                sp.dma_start(raw[:, 1:TILES, SEQ:NI], item_tiles[:, 1:TILES, :]).then_inc(idx_rest_loaded, 16)
                sp.dma_start(raw[:, 1:TILES, NI:NX], sparse_tiles[:, 1:TILES, :]).then_inc(idx_rest_loaded, 16)
                sp.dma_start(dense_rows[:, :, :], dense.rearrange("(t p) n -> p t n", p=P)).then_inc(ffn_weights_loaded, 16)
                for c, (first, k) in enumerate(CHUNKS):
                    sp.dma_start(fw1[0:k, c, :], ffn_w1[first:first + k, :]).then_inc(ffn_weights_loaded, 16)
                    for v, vector in enumerate((bn_gamma, bn_beta, bn_mean, bn_var)):
                        sp.dma_start(bn[0:k, v, c:c + 1], vector[first:first + k].rearrange("(p o) -> p o", o=1))\
                            .then_inc(ffn_weights_loaded, 16)
                for tile, vector in ((fb1, ffn_b1), (fa1, ffn_a1), (fb2, ffn_b2), (fa2, ffn_a2), (ob, out_b)):
                    sp.dma_start(tile[:, :], vector.rearrange("(p o) -> p o", o=1)).then_inc(ffn_weights_loaded, 16)
                sp.dma_start(fw2[:, :], ffn_w2).then_inc(ffn_weights_loaded, 16)
                sp.dma_start(ow[:, :], out_w).then_inc(ffn_weights_loaded, 16)
            sp.wait_ge(score_ready, TILES)
            sp.dma_start(out.rearrange("r o -> o r"), score[:, :]).then_inc(stored, 16)
            sp.wait_ge(stored, 16)

        ATT_LOADS = 16 * 8
        FFN_LOADS = 16 * (1 + 5 * len(CHUNKS) + 7)

        @block.gpsimd
        def _(gp):
            gp.memset(ident[:, :], 0.0).then_inc(ident_zeroed, 1)
            gp.wait_ge(ident_zeroed, 1)
            gp.affine_select(out=ident[:, :], in_=ident[:, :], compare_op=ALU.not_equal, fill=1.0, base=0,
                             pattern=[[-1, P]], channel_multiplier=1).then_inc(ident_ready, 1)

            def gather(rows, table, index, landed):
                gp.indirect_dma_start(rows, None, table, bass.IndirectOffsetOnAxis(ap=index, axis=0)).then_inc(landed, 16)

            with gp.Fori(0, PAIRS) as pair:
                for half in range(2):
                    tile = pair * 2 + half
                    wait(gp, idx_ready, tile + 1)
                    wait(gp, tile_consumed, tile + 1)
                    for n in range(NB):
                        gather(items[:, half, n * E:(n + 1) * E], seq_table, idx[half][:, SEQ + n:SEQ + n + 1],
                               items_landed[half])
                    for g in range(GROUPS):
                        for k in range(G * NB):
                            if g > 0 and k == 6:
                                gp.wait_ge(group_landed[(g - 1) % 2], 16 * G * NB * (tile * (GROUPS // 2) + (g - 1) // 2 + 1))
                                gp.nop(nofuse=True).then_inc(group_ready, 1)
                            c = g * G * NB + k
                            gather(hist[:, half, c * E:(c + 1) * E], seq_table, idx[half][:, c:c + 1], group_landed[g % 2])
                    for n in range(NS):
                        gather(sparse_rows[:, half, n * E:(n + 1) * E], sparse_table, idx[half][:, NI + n:NI + n + 1],
                               sparse_landed[half])
                    gp.wait_ge(group_landed[(GROUPS - 1) % 2], 16 * G * NB * (tile + 1) * (GROUPS // 2))
                    gp.nop(nofuse=True).then_inc(group_ready, 1)

        @block.tensor
        def _(pe):
            pe.sem_inc(tile_consumed, 2)
            pe.wait_ge(ident_ready, 1)
            pe.wait_ge(att_weights_loaded, ATT_LOADS)
            pe.wait_ge(w1_ready, 1)

            with pe.Fori(0, PAIRS) as pair:
                for half in range(2):
                    tile = pair * 2 + half
                    base = tile * GROUPS

                    def turn_group(g):
                        pe.wait_ge(group_ready, base + (g + 1))
                        for j in range(G):
                            step = g * G + j
                            last = nc.tensor.transpose(turned[g % 2][:, j * P:(j + 1) * P],
                                                       hist[:, half, step * D:(step + 1) * D], ident[:, :])
                        last.then_inc(group_turned, 1)

                    def layer1(g):
                        pe.wait_ge(group_copied, base + (g + 1))
                        nc.tensor.matmul(pre1[g % 2][0:A1, :], w1_hist[:, :], hist_t[:, g % 2, :], start=True, stop=False)
                        pe.wait_ge(product_ready, base + (g + 1))
                        nc.tensor.matmul(pre1[g % 2][0:A1, :], w1_prod, prod_t[:, g % 2, :], start=False, stop=True)\
                            .then_inc(layer1_done, 1)

                    def layer2(g):
                        pe.wait_ge(hidden1_ready, base + (g + 1))
                        for k in range(2):
                            last = nc.tensor.matmul(pre2[UP * k:UP * (k + 1), 0:N // 2], w2[:, :],
                                                    hidden1[:, g % 2, k * N // 2:(k + 1) * N // 2], start=True, stop=True)
                        last.then_inc(layer2_done, 1)

                    def logits_of(g):
                        pe.wait_ge(hidden2_ready, base + (g + 1))
                        for j in range(2):
                            last = nc.tensor.matmul(logits[:, g * G + 2 * j:g * G + 2 * j + 2],
                                                    hidden2[:, j * P:(j + 1) * P], wf[:, :], start=True, stop=True)
                        return last

                    pe.wait_ge(items_landed[half], 16 * NB * (pair + 1))
                    nc.tensor.transpose(small[:, 0:P], items[:, half, :], ident[:, :]).then_inc(item_turned, 1)
                    pe.wait_ge(item_copied, tile + 1)
                    nc.tensor.matmul(small[0:A1, P:2 * P], w1_item[:, :], item_t[:, :], start=True, stop=True)\
                        .then_inc(item_part_done, 1)

                    turn_group(0)
                    for g in range(GROUPS):
                        if g + 1 < GROUPS:
                            turn_group(g + 1)
                        layer1(g)
                        if g >= 2:
                            logits_of(g - 2)
                        if g >= 1:
                            layer2(g - 1)
                    logits_of(GROUPS - 2)
                    layer2(GROUPS - 1)
                    logits_of(GROUPS - 1).then_inc(logits_done, 1)

                    pe.wait_ge(ffn_weights_loaded, FFN_LOADS)
                    pe.wait_ge(item_part_ready, tile + 1)
                    pe.wait_ge(sparse_landed[half], 16 * NS * (pair + 1))
                    nc.tensor.transpose(small[:, 0:P], sparse_rows[:, half, 0:2 * E], ident[:, :])
                    nc.tensor.transpose(small[0:SPARSE_B[1], P:2 * P], sparse_rows[:, half, 2 * E:NS * E], ident[:, :])
                    pe.wait_ge(dense_ready, tile + 1)
                    nc.tensor.transpose(small[0:ND, 2 * P:3 * P], dense_now[:, :], ident[:, :])\
                        .then_inc(side_turned, 1)
                    pe.wait_ge(side_copied, tile + 1)
                    pe.wait_ge(user_ready, tile + 1)
                    nc.tensor.transpose(small[:, 3 * P:4 * P], user[:, :], ident[:, :]).then_inc(user_turned, 1)
                    pe.wait_ge(user_copied, tile + 1)
                    pe.sem_inc(tile_consumed, 1)
                    for c, (_, k) in enumerate(CHUNKS):
                        last = nc.tensor.matmul(small[0:H1, 0:P], fw1[0:k, c, :], x[0:k, c, :], start=(c == 0),
                                                stop=(c == len(CHUNKS) - 1))
                    last.then_inc(ffn1_done, 1)
                    pe.wait_ge(y1_ready, tile + 1)
                    nc.tensor.matmul(small[0:H2, 0:P], fw2[:, :], y1[:, :], start=True, stop=True).then_inc(ffn2_done, 1)
                    wait(pe, y2_ready, tile + 1)
                    nc.tensor.matmul(small[0:1, 0:P], ow[:, :], y2[:, :], start=True, stop=True).then_inc(score_done, 1)
                    pe.wait_ge(score_ready, tile + 1)

        @block.scalar
        def _(act):
            act.wait_ge(ffn_weights_loaded, FFN_LOADS)
            act.wait_ge(padded, 1)
            nc.scalar.activation(std[:, :], bn[:, 3, :], ACT.Sqrt, bias=eps[:, :]).then_inc(std_ready, 1)
            act.wait_ge(bn_ready, 1)

            def normalised(c, region):
                k = CHUNKS[c][1]
                return nc.scalar.activation(x[0:k, c, :], region, ACT.Identity, scale=bn_scale[0:k, c:c + 1],
                                            bias=bn_shift[0:k, c:c + 1])

            with act.Fori(0, PAIRS) as pair:
                for half in range(2):
                    tile = pair * 2 + half
                    base = tile * GROUPS

                    def copy_group(g, slot):
                        act.wait_ge(group_turned, base + (g + 1))
                        nc.scalar.copy(hist_t[:, slot, :], turned[slot][:, :]).then_inc(group_copied, 1)

                    def sigmoid1(g, slot):
                        act.wait_ge(item_added, base + (g + 1))
                        nc.scalar.activation(hidden1[:, slot, :], pre1[slot][0:A1, :], ACT.Sigmoid).then_inc(hidden1_ready, 1)

                    def sigmoid2(g):
                        act.wait_ge(layer2_done, base + (g + 1))
                        nc.scalar.activation(hidden2[:, :], pre2[:, 0:N // 2], ACT.Sigmoid, bias=b2[:, :])\
                            .then_inc(hidden2_ready, 1)

                    act.wait_ge(item_turned, tile + 1)
                    normalised(1, small[:, 0:P])
                    nc.scalar.copy(item_t[:, :], small[:, 0:P]).then_inc(item_copied, 1)
                    act.wait_ge(item_part_done, tile + 1)
                    nc.scalar.activation(item_part[:, :], small[0:A1, P:2 * P], ACT.Identity, bias=b1[:, :])\
                        .then_inc(item_part_ready, 1)

                    copy_group(0, 0)
                    copy_group(1, 1)
                    sigmoid1(0, 0)
                    copy_group(2, 0)
                    sigmoid1(1, 1)
                    with act.Fori(0, (GROUPS - 4) // 2) as step:
                        for s in range(2):
                            g = step * 2 + (2 + s)
                            sigmoid2(g - 2)
                            copy_group(g + 1, 1 - s)
                            sigmoid1(g, s)
                    sigmoid2(GROUPS - 4)
                    copy_group(GROUPS - 1, 1)
                    sigmoid1(GROUPS - 2, 0)
                    sigmoid2(GROUPS - 3)
                    sigmoid1(GROUPS - 1, 1)
                    sigmoid2(GROUPS - 2)
                    sigmoid2(GROUPS - 1)

                    act.wait_ge(max_ready, tile + 1)
                    nc.scalar.activation(weight[:, :], logit[:, :], ACT.Exp, bias=neg_max[:, :], accum_out=total[:, :])\
                        .then_inc(weights_ready, 1)
                    act.wait_ge(side_turned, tile + 1)
                    normalised(3, small[:, 0:P])
                    normalised(4, small[0:SPARSE_B[1], P:2 * P])
                    normalised(2, small[0:ND, 2 * P:3 * P]).then_inc(side_copied, 1)
                    act.wait_ge(user_turned, tile + 1)
                    normalised(0, small[:, 3 * P:4 * P]).then_inc(user_copied, 1)
                    act.wait_ge(ffn1_done, tile + 1)
                    nc.scalar.activation(z1[:, :], small[0:H1, 0:P], ACT.Identity, bias=fb1[:, :]).then_inc(z1_ready, 1)
                    act.wait_ge(ffn2_done, tile + 1)
                    nc.scalar.activation(z2[:, :], small[0:H2, 0:P], ACT.Identity, bias=fb2[:, :]).then_inc(z2_ready, 1)
                    wait(act, score_done, tile + 1)
                    nc.scalar.activation(score[:, bass.ds(tile * P, P)], small[0:1, 0:P], ACT.Sigmoid, bias=ob[:, :])\
                        .then_inc(score_ready, 1)

        @block.vector
        def _(dve):
            nc.vector.memset(w2[:, :], 0.0)
            nc.vector.memset(b2[:, :], 0.0)
            nc.vector.memset(wf[:, :], 0.0)
            nc.vector.memset(bn[:, :, :], 1.0)
            nc.vector.memset(raw[:, TILES, :], 0)
            nc.vector.memset(masked_logit[:, :], MASKED)
            nc.vector.memset(eps[:, :], BN_EPS)
            for n in range(NB):
                nc.vector.memset(table_start[:, n:NI:NB], float(n * V))
            for n in range(NS):
                last = nc.vector.memset(table_start[:, NI + n:NI + n + 1], float(n * V))
            last.then_inc(padded, 1)
            dve.wait_ge(padded, 1)

            def row_numbers(tile, half):
                before = tile * 3
                nc.vector.tensor_scalar(wrap[:, :], raw[:, tile, :], 0.0, float(V), ALU.is_lt, ALU.mult).then_inc(idx_step, 1)
                dve.wait_ge(idx_step, before + 1)
                nc.vector.tensor_tensor(wrap[:, :], wrap[:, :], raw[:, tile, :], ALU.add).then_inc(idx_step, 1)
                dve.wait_ge(idx_step, before + 2)
                nc.vector.tensor_scalar(wrap[:, :], wrap[:, :], 0.0, float(V - 1), ALU.max, ALU.min).then_inc(idx_step, 1)
                dve.wait_ge(idx_step, before + 3)
                nc.vector.tensor_tensor(idx[half][:, :], wrap[:, :], table_start[:, :], ALU.add).then_inc(idx_ready, 1)
                nc.vector.tensor_scalar(masked[half][:, :].rearrange("p (g j k) -> p g j k", j=2, k=2),
                                        raw[:, tile, 0:SEQ:NB].rearrange("p (g k j) -> p g j k", k=2, j=2),
                                        0.0, None, ALU.is_equal)

            dve.wait_ge(idx_loaded, 48)
            row_numbers(0, 0)

            dve.wait_ge(att_weights_loaded, ATT_LOADS)
            nc.vector.tensor_tensor(w1_item[:, :], w1_raw[:, 0, :], w1_raw[:, 2, :], ALU.add)
            nc.vector.tensor_tensor(w1_hist[:, :], w1_raw[:, 1, :], w1_raw[:, 2, :], ALU.subtract).then_inc(w1_ready, 1)

            v, r, t = (bn_x[:, i, :] for i in range(3))
            steps = [0]

            def settled(instruction):
                steps[0] += 1
                instruction.then_inc(bn_step, 1)
                dve.wait_ge(bn_step, steps[0])

            dve.wait_ge(ffn_weights_loaded, FFN_LOADS)
            settled(nc.vector.tensor_scalar(v, bn[:, 3, :], BN_EPS, None, ALU.add))
            dve.wait_ge(std_ready, 1)
            settled(nc.vector.reciprocal(r, std[:, :]))
            settled(nc.vector.tensor_tensor(t, r, r, ALU.mult))
            settled(nc.vector.tensor_tensor(t, t, v, ALU.mult))
            settled(nc.vector.tensor_scalar(t, t, -0.5, 1.5, ALU.mult, ALU.add))
            settled(nc.vector.tensor_tensor(r, r, t, ALU.mult))
            settled(nc.vector.tensor_tensor(bn_scale[:, :], bn[:, 0, :], r, ALU.mult))
            settled(nc.vector.tensor_tensor(t, bn[:, 2, :], bn_scale[:, :], ALU.mult))
            nc.vector.tensor_tensor(bn_shift[:, :], bn[:, 1, :], t, ALU.subtract).then_inc(bn_ready, 1)

            dve.wait_ge(idx_rest_loaded, 48)
            with dve.Fori(0, PAIRS) as pair:
                for half in range(2):
                    tile = pair * 2 + half
                    base = tile * GROUPS

                    def product(g, slot):
                        dve.wait_ge(group_copied, base + (g + 1))
                        nc.vector.tensor_tensor(prod_t[:, slot, :].rearrange("p (l b) -> p l b", b=P),
                                                turned[slot][:, :].rearrange("p (l b) -> p l b", b=P),
                                                item_t[:, :].unsqueeze(1).broadcast_to([P, G, P]), ALU.mult)\
                            .then_inc(product_ready, 1)

                    def add_item(g, slot):
                        dve.wait_ge(layer1_done, base + (g + 1))
                        columns = pre1[slot][0:A1, :].rearrange("p (l b) -> p l b", b=P)
                        nc.vector.tensor_tensor(columns, columns, item_part[:, :].unsqueeze(1).broadcast_to([A1, G, P]),
                                                ALU.add).then_inc(item_added, 1)

                    row_numbers(tile + 1, 1 - half)

                    nc.vector.tensor_copy(dense_now[:, :], dense_rows[:, tile, :]).then_inc(dense_ready, 1)
                    wait(dve, item_copied, tile + 1)
                    product(0, 0)
                    product(1, 1)
                    wait(dve, item_part_ready, tile + 1)
                    add_item(0, 0)
                    product(2, 0)
                    add_item(1, 1)
                    with dve.Fori(0, (GROUPS - 4) // 2) as step:
                        for s in range(2):
                            g = step * 2 + (2 + s)
                            product(g + 1, 1 - s)
                            add_item(g, s)
                    product(GROUPS - 1, 1)
                    add_item(GROUPS - 2, 0)
                    add_item(GROUPS - 1, 1)

                    dve.wait_ge(logits_done, tile + 1)
                    nc.vector.tensor_scalar(logit[:, :], logits[:, 0:L], bf[:, :], None, ALU.add).then_inc(softmax_step, 1)
                    wait(dve, softmax_step, tile * 2 + 1)
                    nc.vector.copy_predicated(logit[:, :], masked[half][:, :], masked_logit[:, :]).then_inc(softmax_step, 1)
                    dve.wait_ge(softmax_step, tile * 2 + 2)
                    nc.vector.tensor_reduce(neg_max[:, :], logit[:, :], AX.X, ALU.max, negate=True).then_inc(max_ready, 1)
                    wait(dve, weights_ready, tile + 1)
                    nc.vector.reciprocal(inv_total[:, :], total[:, :])

                    before = tile * L

                    def add_step(g, k):
                        row = hist[:, half, bass.ds((g * G + k) * D, D)]
                        by = weight[:, bass.ds(g * G + (k // 2 + 2 * (k % 2)), 1)]
                        acc = odd_acc if k % 2 else even_acc
                        if isinstance(g, int) and g == 0 and k < 2:
                            nc.vector.tensor_scalar(acc, row, by, None, ALU.mult).then_inc(sum_step, 1)
                        else:
                            dve.wait_ge(sum_step, before + (g * G + (k - 1)))
                            nc.vector.scalar_tensor_tensor(acc, row, by, acc, ALU.mult, ALU.add).then_inc(sum_step, 1)

                    for k in range(G):
                        add_step(0, k)
                    with dve.Fori(1, GROUPS) as g:
                        for k in range(G):
                            add_step(g, k)
                    dve.wait_ge(sum_step, before + L)
                    nc.vector.tensor_scalar(odd_sum[:, :], odd_acc, inv_total[:, :], None, ALU.mult).then_inc(user_step, 1)
                    dve.wait_ge(user_step, tile + 1)
                    nc.vector.scalar_tensor_tensor(user[:, :], even_acc, inv_total[:, :], odd_sum[:, :], ALU.mult, ALU.add)\
                        .then_inc(user_ready, 1)

                    dve.wait_ge(z1_ready, tile + 1)
                    nc.vector.tensor_scalar(n1[:, :], z1[:, :], 0.0, fa1[:, :], ALU.min, ALU.mult).then_inc(n1_ready, 1)
                    dve.wait_ge(n1_ready, tile + 1)
                    nc.vector.scalar_tensor_tensor(y1[:, :], z1[:, :], 0.0, n1[:, :], ALU.max, ALU.add).then_inc(y1_ready, 1)
                    dve.wait_ge(z2_ready, tile + 1)
                    nc.vector.tensor_scalar(n2[:, :], z2[:, :], 0.0, fa2[:, :], ALU.min, ALU.mult).then_inc(n2_ready, 1)
                    dve.wait_ge(n2_ready, tile + 1)
                    nc.vector.scalar_tensor_tensor(y2[:, :], z2[:, :], 0.0, n2[:, :], ALU.max, ALU.add).then_inc(y2_ready, 1)


INPUTS = ["r_dense_inputs", "r_sparse_inputs", "r_seq_inputs", "r_item_inputs", "L0_rec_emb_sparse", "L0_rec_emb_seq",
          "L0_rec_att_W1", "L0_rec_att_b1", "L0_rec_att_W2", "L0_rec_att_b2", "L0_rec_att_Wf", "L0_rec_att_bf",
          "L0_rec_bn_gamma", "L0_rec_bn_beta", "L0_rec_bn_mean", "L0_rec_bn_var", "L0_rec_ffn_W1", "L0_rec_ffn_b1",
          "L0_rec_ffn_a1", "L0_rec_ffn_W2", "L0_rec_ffn_b2", "L0_rec_ffn_a2", "L0_rec_out_W", "L0_rec_out_b"]


def kernel(**inputs):
    import numpy as _np
    import concourse.bacc as _bacc
    from concourse import mybir as _mybir
    from concourse.bass_utils import run_bass_kernel_spmd as _run

    nc = _bacc.Bacc("TRN2", target_bir_lowering=False, num_devices=1)
    arrays, args = {}, []
    for name in INPUTS:
        a = _np.ascontiguousarray(inputs[name])
        arrays[f"in_{name}_dram"] = a
        args.append(nc.dram_tensor(f"in_{name}_dram", a.shape, _mybir.dt.from_np(a.dtype), kind="ExternalInput").ap())
    rows = inputs["r_dense_inputs"].shape[0]
    args.append(nc.dram_tensor("out_0_dram", (rows, 1), _mybir.dt.float32, kind="ExternalOutput").ap())
    build(nc, *args)
    r = _run(nc, [arrays], core_ids=[0])
    return r.results[0]["out_0_dram"]
```

```python
from contextlib import ExitStack

import concourse.bass as bass
from concourse import mybir

F32 = mybir.dt.float32
I32 = mybir.dt.int32
ALU = mybir.AluOpType
ACT = mybir.ActivationFunctionType
AX = mybir.AxisListType

P = 128
MASKED = -2.0 ** 32 + 1
BN_EPS = 0.001


def build(nc, dense, sparse, seq, item, emb_sparse, emb_seq, att_w1, att_b1, att_w2, att_b2, att_wf, att_bf,
          bn_gamma, bn_beta, bn_mean, bn_var, ffn_w1, ffn_b1, ffn_a1, ffn_w2, ffn_b2, ffn_a2, out_w, out_b, identity, out):
    ROWS, L, NB = seq.shape
    V, E = emb_seq.shape[1:]
    NS, ND = sparse.shape[1], dense.shape[1]
    D = NB * E
    A1, A2 = att_w2.shape
    H1, H2 = ffn_w2.shape
    TILES = ROWS // P
    PAIRS = TILES // 2
    G = 4
    GROUPS = L // G
    N = G * P
    SEQ, NI = L * NB, L * NB + NB
    NX = NI + NS
    EARLY = 7
    UP = 64
    assert D == P and A2 <= UP and TILES % 2 == 0 and GROUPS % 2 == 0 and EARLY == 7 and GROUPS == 10

    seq_table = emb_seq.rearrange("n v e -> (n v) e")
    sparse_table = emb_sparse.rearrange("n v e -> (n v) e")
    USER, ITEM, DENSE = (0, D), (D, D), (2 * D, ND)
    SPARSE_A, SPARSE_B = (2 * D + ND, 2 * E), (2 * D + ND + 2 * E, (NS - 2) * E)
    CHUNKS = [USER, ITEM, DENSE, SPARSE_A, SPARSE_B]

    ctx = ExitStack()
    with ctx:
        def sb(name, shape, dt=F32):
            return ctx.enter_context(nc.sbuf_tensor(name, shape, dt))

        def ps(name):
            return ctx.enter_context(nc.psum_tensor(name, [P, 512], F32))

        def sem(name):
            return ctx.enter_context(nc.semaphore(name))

        raw = sb("raw", [P, TILES + 1, NX], I32)
        wrap = sb("wrap", [P, NX])
        table_start = sb("table_start", [P, NX])
        idx = [sb(f"idx{h}", [P, NX], I32) for h in range(2)]
        masked = [sb(f"masked{h}", [P, L], I32) for h in range(2)]
        masked_logit = sb("masked_logit", [P, L])
        hist = sb("hist", [P, 2, L * D])
        items = sb("items", [P, 2, D])
        sparse_rows = sb("sparse_rows", [P, 2, NS * E])
        dense_rows = sb("dense_rows", [P, TILES, ND])
        dense_now = sb("dense_now", [P, ND])
        ident = sb("ident", [P, P])
        w1_raw = sb("w1_raw", [P, 4, A1])
        w1_item = sb("w1_item", [P, A1])
        w1_hist = sb("w1_hist", [P, A1])
        w1_prod = w1_raw[:, 3, :]
        b1 = sb("b1", [A1, 1])
        w2 = sb("w2", [A1, UP])
        b2 = sb("b2", [P, 1])
        wf = sb("wf", [P, 2])
        bf = sb("bf", [P, 1])
        fw1 = sb("fw1", [P, len(CHUNKS), H1])
        fb1 = sb("fb1", [H1, 1])
        fa1 = sb("fa1", [H1, 1])
        fw2 = sb("fw2", [H1, H2])
        fb2 = sb("fb2", [H2, 1])
        fa2 = sb("fa2", [H2, 1])
        ow = sb("ow", [H2, 1])
        ob = sb("ob", [1, 1])
        bn = sb("bn", [P, 4, len(CHUNKS)])
        bn_x = sb("bn_x", [P, 3, len(CHUNKS)])
        std = sb("std", [P, len(CHUNKS)])
        eps = sb("eps", [P, 1])
        bn_scale = sb("bn_scale", [P, len(CHUNKS)])
        bn_shift = sb("bn_shift", [P, len(CHUNKS)])
        hist_t = sb("hist_t", [P, 2, N])
        prod_t = sb("prod_t", [P, 2, N])
        hidden1 = sb("hidden1", [A1, 2, N])
        hidden2 = sb("hidden2", [P, N // 2])
        item_t = sb("item_t", [P, P])
        item_part = sb("item_part", [A1, P])
        logit = sb("logit", [P, L])
        neg_max_early = sb("neg_max_early", [P, 1])
        neg_max_late = sb("neg_max_late", [P, 1])
        neg_max = sb("neg_max", [P, 1])
        weight = sb("weight", [P, L])
        total_early = sb("total_early", [P, 1])
        total_late = sb("total_late", [P, 1])
        rescale = sb("rescale", [P, 1])
        total = sb("total", [P, 1])
        inv_total = sb("inv_total", [P, 1])
        early_sum = sb("early_sum", [P, D])
        odd_sum = sb("odd_sum", [P, D])
        user = sb("user", [P, D])
        x = sb("x", [P, len(CHUNKS), P])
        z1 = sb("z1", [H1, P])
        n1 = sb("n1", [H1, P])
        y1 = sb("y1", [H1, P])
        z2 = sb("z2", [H2, P])
        n2 = sb("n2", [H2, P])
        y2 = sb("y2", [H2, P])
        score = sb("score", [1, ROWS])

        turned = [ps(f"turned{s}") for s in range(2)]
        pre1 = [ps(f"pre1{s}") for s in range(2)]
        pre2 = ps("pre2")
        logits = ps("logits")
        small = ps("small")
        sums = ps("sums")
        even_acc, odd_acc = sums[:, 0:D], sums[:, D:2 * D]

        idx_loaded = sem("idx_loaded")
        idx_rest_loaded = sem("idx_rest_loaded")
        att_weights_loaded = sem("att_weights_loaded")
        ffn_weights_loaded = sem("ffn_weights_loaded")
        stored = sem("stored")
        padded = sem("padded")
        dense_ready = sem("dense_ready")
        ident_ready = sem("ident_ready")
        w1_ready = sem("w1_ready")
        bn_step = sem("bn_step")
        bn_ready = sem("bn_ready")
        std_ready = sem("std_ready")
        idx_ready = sem("idx_ready")
        idx_step = sem("idx_step")
        items_landed = [sem(f"items_landed{h}") for h in range(2)]
        sparse_landed = [sem(f"sparse_landed{h}") for h in range(2)]
        group_landed = [sem(f"group_landed{s}") for s in range(2)]
        group_ready = sem("group_ready")
        tile_consumed = sem("tile_consumed")
        group_turned = sem("group_turned")
        group_copied = sem("group_copied")
        product_ready = sem("product_ready")
        layer1_done = sem("layer1_done")
        item_added = sem("item_added")
        hidden1_ready = sem("hidden1_ready")
        layer2_done = sem("layer2_done")
        hidden2_ready = sem("hidden2_ready")
        item_turned = sem("item_turned")
        item_copied = sem("item_copied")
        item_part_done = sem("item_part_done")
        item_part_ready = sem("item_part_ready")
        logits_done = sem("logits_done")
        softmax_step = sem("softmax_step")
        early_logits_done = sem("early_logits_done")
        early_max_ready = sem("early_max_ready")
        early_weights_ready = sem("early_weights_ready")
        early_sum_step = sem("early_sum_step")
        max_ready = sem("max_ready")
        weights_ready = sem("weights_ready")
        merge_step = sem("merge_step")
        sum_step = sem("sum_step")
        user_step = sem("user_step")
        user_ready = sem("user_ready")
        side_turned = sem("side_turned")
        side_copied = sem("side_copied")
        user_turned = sem("user_turned")
        user_copied = sem("user_copied")
        ffn1_done = sem("ffn1_done")
        z1_ready = sem("z1_ready")
        n1_ready = sem("n1_ready")
        y1_ready = sem("y1_ready")
        ffn2_done = sem("ffn2_done")
        z2_ready = sem("z2_ready")
        n2_ready = sem("n2_ready")
        y2_ready = sem("y2_ready")
        score_done = sem("score_done")
        score_ready = sem("score_ready")

        def wait(eng, semaphore, count):
            eng.wait_ge(semaphore, count)
            eng.nop(nofuse=True)

        block = ctx.enter_context(nc.Block())

        @block.sync
        def _(sp):
            seq_t = seq.rearrange("(t p) l n -> p t (l n)", p=P)
            item_tiles = item.rearrange("(t p) n -> p t n", p=P)
            sparse_tiles = sparse.rearrange("(t p) n -> p t n", p=P)
            with nc.allow_non_contiguous_dma(reason="short index rows and vectors by partition"):
                sp.dma_start(raw[:, 0, 0:SEQ], seq_t[:, 0, :]).then_inc(idx_loaded, 16)
                sp.dma_start(raw[:, 0, SEQ:NI], item_tiles[:, 0, :]).then_inc(idx_loaded, 16)
                sp.dma_start(raw[:, 0, NI:NX], sparse_tiles[:, 0, :]).then_inc(idx_loaded, 16)
                sp.dma_start(ident[:, :], identity).then_inc(ident_ready, 16)
                sp.dma_start(w1_raw[:, :, :], att_w1.rearrange("(c p) n -> p c n", p=P)).then_inc(att_weights_loaded, 16)
                sp.dma_start(b1[:, :], att_b1.rearrange("(p o) -> p o", o=1)).then_inc(att_weights_loaded, 16)
                sp.wait_ge(padded, 1)
                sp.dma_start(w2[:, 0:A2], att_w2).then_inc(att_weights_loaded, 16)
                for half in range(2):
                    rows = slice(UP * half, UP * half + A2)
                    sp.dma_start(b2[rows, :], att_b2.rearrange("(p o) -> p o", o=1)).then_inc(att_weights_loaded, 16)
                    sp.dma_start(wf[rows, half:half + 1], att_wf).then_inc(att_weights_loaded, 16)
                sp.dma_start(bf[:, :], att_bf.rearrange("(p o) -> p o", o=1).broadcast_to([P, 1]))\
                    .then_inc(att_weights_loaded, 16)
                sp.dma_start(raw[:, 1:TILES, 0:SEQ], seq_t[:, 1:TILES, :]).then_inc(idx_rest_loaded, 16)
                sp.dma_start(raw[:, 1:TILES, SEQ:NI], item_tiles[:, 1:TILES, :]).then_inc(idx_rest_loaded, 16)
                sp.dma_start(raw[:, 1:TILES, NI:NX], sparse_tiles[:, 1:TILES, :]).then_inc(idx_rest_loaded, 16)
                sp.dma_start(dense_rows[:, :, :], dense.rearrange("(t p) n -> p t n", p=P)).then_inc(ffn_weights_loaded, 16)
                for c, (first, k) in enumerate(CHUNKS):
                    sp.dma_start(fw1[0:k, c, :], ffn_w1[first:first + k, :]).then_inc(ffn_weights_loaded, 16)
                    for v, vector in enumerate((bn_gamma, bn_beta, bn_mean, bn_var)):
                        sp.dma_start(bn[0:k, v, c:c + 1], vector[first:first + k].rearrange("(p o) -> p o", o=1))\
                            .then_inc(ffn_weights_loaded, 16)
                for tile, vector in ((fb1, ffn_b1), (fa1, ffn_a1), (fb2, ffn_b2), (fa2, ffn_a2), (ob, out_b)):
                    sp.dma_start(tile[:, :], vector.rearrange("(p o) -> p o", o=1)).then_inc(ffn_weights_loaded, 16)
                sp.dma_start(fw2[:, :], ffn_w2).then_inc(ffn_weights_loaded, 16)
                sp.dma_start(ow[:, :], out_w).then_inc(ffn_weights_loaded, 16)
            sp.wait_ge(score_ready, TILES)
            sp.dma_start(out.rearrange("r o -> o r"), score[:, :]).then_inc(stored, 16)
            sp.wait_ge(stored, 16)

        ATT_LOADS = 16 * 8
        FFN_LOADS = 16 * (1 + 5 * len(CHUNKS) + 7)

        @block.gpsimd
        def _(gp):
            def gather(rows, table, index, landed):
                gp.indirect_dma_start(rows, None, table, bass.IndirectOffsetOnAxis(ap=index, axis=0)).then_inc(landed, 16)

            with gp.Fori(0, PAIRS) as pair:
                for half in range(2):
                    tile = pair * 2 + half
                    wait(gp, idx_ready, tile + 1)
                    wait(gp, tile_consumed, tile + 1)
                    for n in range(NB):
                        gather(items[:, half, n * E:(n + 1) * E], seq_table, idx[half][:, SEQ + n:SEQ + n + 1],
                               items_landed[half])
                    for g in range(GROUPS):
                        for k in range(G * NB):
                            if g > 0 and k == 6:
                                gp.wait_ge(group_landed[(g - 1) % 2], 16 * G * NB * (tile * (GROUPS // 2) + (g - 1) // 2 + 1))
                                gp.nop(nofuse=True).then_inc(group_ready, 1)
                            c = g * G * NB + k
                            gather(hist[:, half, c * E:(c + 1) * E], seq_table, idx[half][:, c:c + 1], group_landed[g % 2])
                    for n in range(NS):
                        gather(sparse_rows[:, half, n * E:(n + 1) * E], sparse_table, idx[half][:, NI + n:NI + n + 1],
                               sparse_landed[half])
                    gp.wait_ge(group_landed[(GROUPS - 1) % 2], 16 * G * NB * (tile + 1) * (GROUPS // 2))
                    gp.nop(nofuse=True).then_inc(group_ready, 1)

        @block.tensor
        def _(pe):
            pe.sem_inc(tile_consumed, 2)
            pe.wait_ge(ident_ready, 16)
            pe.wait_ge(att_weights_loaded, ATT_LOADS)
            pe.wait_ge(w1_ready, 1)

            with pe.Fori(0, PAIRS) as pair:
                for half in range(2):
                    tile = pair * 2 + half
                    base = tile * GROUPS

                    def turn_group(g):
                        if g < GROUPS - 1:
                            pe.wait_ge(group_ready, base + (g + 1))
                        else:
                            pe.wait_ge(group_landed[g % 2], 16 * G * NB * (tile + 1) * (GROUPS // 2))
                        for j in range(G):
                            step = g * G + j
                            last = nc.tensor.transpose(turned[g % 2][:, j * P:(j + 1) * P],
                                                       hist[:, half, step * D:(step + 1) * D], ident[:, :])
                        last.then_inc(group_turned, 1)

                    def layer1(g):
                        pe.wait_ge(group_copied, base + (g + 1))
                        nc.tensor.matmul(pre1[g % 2][0:A1, :], w1_hist[:, :], hist_t[:, g % 2, :], start=True, stop=False)
                        pe.wait_ge(product_ready, base + (g + 1))
                        nc.tensor.matmul(pre1[g % 2][0:A1, :], w1_prod, prod_t[:, g % 2, :], start=False, stop=True)\
                            .then_inc(layer1_done, 1)

                    def layer2(g):
                        pe.wait_ge(hidden1_ready, base + (g + 1))
                        for k in range(2):
                            last = nc.tensor.matmul(pre2[UP * k:UP * (k + 1), 0:N // 2], w2[:, :],
                                                    hidden1[:, g % 2, k * N // 2:(k + 1) * N // 2], start=True, stop=True)
                        last.then_inc(layer2_done, 1)

                    def logits_of(g):
                        pe.wait_ge(hidden2_ready, base + (g + 1))
                        for j in range(2):
                            last = nc.tensor.matmul(logits[:, g * G + 2 * j:g * G + 2 * j + 2],
                                                    hidden2[:, j * P:(j + 1) * P], wf[:, :], start=True, stop=True)
                        return last

                    pe.wait_ge(items_landed[half], 16 * NB * (pair + 1))
                    nc.tensor.transpose(small[:, 0:P], items[:, half, :], ident[:, :]).then_inc(item_turned, 1)
                    pe.wait_ge(item_copied, tile + 1)
                    nc.tensor.matmul(small[0:A1, P:2 * P], w1_item[:, :], item_t[:, :], start=True, stop=True)\
                        .then_inc(item_part_done, 1)

                    turn_group(0)
                    for g in range(EARLY):
                        if g + 1 < EARLY:
                            turn_group(g + 1)
                        layer1(g)
                        if g >= 2:
                            logits_of(g - 2)
                        if g >= 1:
                            layer2(g - 1)
                    logits_of(EARLY - 2)
                    layer2(EARLY - 1)
                    logits_of(EARLY - 1).then_inc(early_logits_done, 1)
                    for g in range(EARLY, GROUPS):
                        if g < GROUPS - 1:
                            turn_group(g)
                        layer1(g)
                        if g == GROUPS - 2:
                            turn_group(g + 1)
                        layer2(g)
                        last = logits_of(g)
                    last.then_inc(logits_done, 1)

                    pe.wait_ge(ffn_weights_loaded, FFN_LOADS)
                    pe.wait_ge(item_part_ready, tile + 1)
                    pe.wait_ge(sparse_landed[half], 16 * NS * (pair + 1))
                    nc.tensor.transpose(small[:, 0:P], sparse_rows[:, half, 0:2 * E], ident[:, :])
                    nc.tensor.transpose(small[0:SPARSE_B[1], P:2 * P], sparse_rows[:, half, 2 * E:NS * E], ident[:, :])
                    pe.wait_ge(dense_ready, tile + 1)
                    nc.tensor.transpose(small[0:ND, 2 * P:3 * P], dense_now[:, :], ident[:, :])\
                        .then_inc(side_turned, 1)
                    pe.wait_ge(side_copied, tile + 1)
                    for c in (1, 2, 3, 4):
                        k = CHUNKS[c][1]
                        nc.tensor.matmul(logits[0:H1, P:2 * P], fw1[0:k, c, :], x[0:k, c, :], start=(c == 1), stop=False)
                    pe.wait_ge(user_ready, tile + 1)
                    nc.tensor.transpose(small[:, 3 * P:4 * P], user[:, :], ident[:, :]).then_inc(user_turned, 1)
                    pe.wait_ge(user_copied, tile + 1)
                    pe.sem_inc(tile_consumed, 1)
                    last = nc.tensor.matmul(logits[0:H1, P:2 * P], fw1[:, 0, :], x[:, 0, :], start=False, stop=True)
                    last.then_inc(ffn1_done, 1)
                    pe.wait_ge(y1_ready, tile + 1)
                    nc.tensor.matmul(small[0:H2, 0:P], fw2[:, :], y1[:, :], start=True, stop=True).then_inc(ffn2_done, 1)
                    wait(pe, y2_ready, tile + 1)
                    nc.tensor.matmul(small[0:1, 0:P], ow[:, :], y2[:, :], start=True, stop=True).then_inc(score_done, 1)
                    pe.wait_ge(score_ready, tile + 1)

        @block.scalar
        def _(act):
            act.wait_ge(ffn_weights_loaded, FFN_LOADS)
            act.wait_ge(padded, 1)
            nc.scalar.activation(std[:, :], bn[:, 3, :], ACT.Sqrt, bias=eps[:, :]).then_inc(std_ready, 1)
            act.wait_ge(bn_ready, 1)

            def normalised(c, region):
                k = CHUNKS[c][1]
                return nc.scalar.activation(x[0:k, c, :], region, ACT.Identity, scale=bn_scale[0:k, c:c + 1],
                                            bias=bn_shift[0:k, c:c + 1])

            with act.Fori(0, PAIRS) as pair:
                for half in range(2):
                    tile = pair * 2 + half
                    base = tile * GROUPS

                    def copy_group(g, slot):
                        act.wait_ge(group_turned, base + (g + 1))
                        nc.scalar.copy(hist_t[:, slot, :], turned[slot][:, :]).then_inc(group_copied, 1)

                    def sigmoid1(g, slot):
                        act.wait_ge(item_added, base + (g + 1))
                        nc.scalar.activation(hidden1[:, slot, :], pre1[slot][0:A1, :], ACT.Sigmoid).then_inc(hidden1_ready, 1)

                    def sigmoid2(g):
                        act.wait_ge(layer2_done, base + (g + 1))
                        nc.scalar.activation(hidden2[:, :], pre2[:, 0:N // 2], ACT.Sigmoid, bias=b2[:, :])\
                            .then_inc(hidden2_ready, 1)

                    act.wait_ge(item_turned, tile + 1)
                    normalised(1, small[:, 0:P])
                    nc.scalar.copy(item_t[:, :], small[:, 0:P]).then_inc(item_copied, 1)
                    act.wait_ge(item_part_done, tile + 1)
                    nc.scalar.activation(item_part[:, :], small[0:A1, P:2 * P], ACT.Identity, bias=b1[:, :])\
                        .then_inc(item_part_ready, 1)

                    copy_group(0, 0)
                    copy_group(1, 1)
                    sigmoid1(0, 0)
                    copy_group(2, 0)
                    sigmoid1(1, 1)
                    with act.Fori(0, (EARLY - 3) // 2) as step:
                        for s in range(2):
                            g = step * 2 + (2 + s)
                            sigmoid2(g - 2)
                            copy_group(g + 1, 1 - s)
                            sigmoid1(g, s)
                    sigmoid2(EARLY - 3)
                    sigmoid1(EARLY - 1, 0)
                    sigmoid2(EARLY - 2)
                    sigmoid2(EARLY - 1)
                    copy_group(EARLY, EARLY % 2)
                    act.preload_act_table(ACT.Exp)
                    act.wait_ge(early_max_ready, tile + 1)
                    nc.scalar.activation(weight[:, 0:EARLY * G], logit[:, 0:EARLY * G], ACT.Exp, bias=neg_max_early[:, :],
                                         accum_out=total_early[:, :]).then_inc(early_weights_ready, 1)
                    act.preload_act_table(ACT.Sigmoid)
                    for g in range(EARLY, GROUPS):
                        sigmoid1(g, g % 2)
                        if g == GROUPS - 2:
                            copy_group(g + 1, 1 - g % 2)
                        sigmoid2(g)
                        if g < GROUPS - 2:
                            copy_group(g + 1, 1 - g % 2)

                    act.preload_act_table(ACT.Exp)
                    act.wait_ge(max_ready, tile + 1)
                    nc.scalar.activation(rescale[:, :], neg_max_early[:, :], ACT.Exp, bias=neg_max[:, :], scale=-1.0)
                    nc.scalar.activation(weight[:, EARLY * G:L], logit[:, EARLY * G:L], ACT.Exp, bias=neg_max[:, :],
                                         accum_out=total_late[:, :]).then_inc(weights_ready, 1)
                    act.preload_act_table(ACT.Sigmoid)
                    act.wait_ge(side_turned, tile + 1)
                    normalised(3, small[:, 0:P])
                    normalised(4, small[0:SPARSE_B[1], P:2 * P])
                    normalised(2, small[0:ND, 2 * P:3 * P]).then_inc(side_copied, 1)
                    act.wait_ge(user_turned, tile + 1)
                    normalised(0, small[:, 3 * P:4 * P]).then_inc(user_copied, 1)
                    act.wait_ge(ffn1_done, tile + 1)
                    nc.scalar.activation(z1[:, :], logits[0:H1, P:2 * P], ACT.Identity, bias=fb1[:, :]).then_inc(z1_ready, 1)
                    act.wait_ge(ffn2_done, tile + 1)
                    nc.scalar.activation(z2[:, :], small[0:H2, 0:P], ACT.Identity, bias=fb2[:, :]).then_inc(z2_ready, 1)
                    wait(act, score_done, tile + 1)
                    nc.scalar.activation(score[:, bass.ds(tile * P, P)], small[0:1, 0:P], ACT.Sigmoid, bias=ob[:, :])\
                        .then_inc(score_ready, 1)

        @block.vector
        def _(dve):
            nc.vector.memset(w2[:, :], 0.0)
            nc.vector.memset(b2[:, :], 0.0)
            nc.vector.memset(wf[:, :], 0.0)
            nc.vector.memset(bn[:, :, :], 1.0)
            nc.vector.memset(raw[:, TILES, :], 0)
            nc.vector.memset(masked_logit[:, :], MASKED)
            nc.vector.memset(eps[:, :], BN_EPS)
            for n in range(NB):
                nc.vector.memset(table_start[:, n:NI:NB], float(n * V))
            for n in range(NS):
                last = nc.vector.memset(table_start[:, NI + n:NI + n + 1], float(n * V))
            last.then_inc(padded, 1)
            dve.wait_ge(padded, 1)

            def row_numbers(tile, half):
                before = tile * 3
                nc.vector.tensor_scalar(wrap[:, :], raw[:, tile, :], 0.0, float(V), ALU.is_lt, ALU.mult).then_inc(idx_step, 1)
                dve.wait_ge(idx_step, before + 1)
                nc.vector.tensor_tensor(wrap[:, :], wrap[:, :], raw[:, tile, :], ALU.add).then_inc(idx_step, 1)
                dve.wait_ge(idx_step, before + 2)
                nc.vector.tensor_scalar(wrap[:, :], wrap[:, :], 0.0, float(V - 1), ALU.max, ALU.min).then_inc(idx_step, 1)
                dve.wait_ge(idx_step, before + 3)
                nc.vector.tensor_tensor(idx[half][:, :], wrap[:, :], table_start[:, :], ALU.add).then_inc(idx_ready, 1)
                nc.vector.tensor_scalar(masked[half][:, :].rearrange("p (g j k) -> p g j k", j=2, k=2),
                                        raw[:, tile, 0:SEQ:NB].rearrange("p (g k j) -> p g j k", k=2, j=2),
                                        0.0, None, ALU.is_equal)

            dve.wait_ge(idx_loaded, 48)
            row_numbers(0, 0)

            dve.wait_ge(att_weights_loaded, ATT_LOADS)
            nc.vector.tensor_tensor(w1_item[:, :], w1_raw[:, 0, :], w1_raw[:, 2, :], ALU.add)
            nc.vector.tensor_tensor(w1_hist[:, :], w1_raw[:, 1, :], w1_raw[:, 2, :], ALU.subtract).then_inc(w1_ready, 1)

            v, r, t = (bn_x[:, i, :] for i in range(3))
            steps = [0]

            def settled(instruction):
                steps[0] += 1
                instruction.then_inc(bn_step, 1)
                dve.wait_ge(bn_step, steps[0])

            dve.wait_ge(ffn_weights_loaded, FFN_LOADS)
            settled(nc.vector.tensor_scalar(v, bn[:, 3, :], BN_EPS, None, ALU.add))
            dve.wait_ge(std_ready, 1)
            settled(nc.vector.reciprocal(r, std[:, :]))
            settled(nc.vector.tensor_tensor(t, r, r, ALU.mult))
            settled(nc.vector.tensor_tensor(t, t, v, ALU.mult))
            settled(nc.vector.tensor_scalar(t, t, -0.5, 1.5, ALU.mult, ALU.add))
            settled(nc.vector.tensor_tensor(r, r, t, ALU.mult))
            settled(nc.vector.tensor_tensor(bn_scale[:, :], bn[:, 0, :], r, ALU.mult))
            settled(nc.vector.tensor_tensor(t, bn[:, 2, :], bn_scale[:, :], ALU.mult))
            nc.vector.tensor_tensor(bn_shift[:, :], bn[:, 1, :], t, ALU.subtract).then_inc(bn_ready, 1)

            dve.wait_ge(idx_rest_loaded, 48)
            with dve.Fori(0, PAIRS) as pair:
                for half in range(2):
                    tile = pair * 2 + half
                    base = tile * GROUPS

                    def product(g, slot):
                        dve.wait_ge(group_copied, base + (g + 1))
                        nc.vector.tensor_tensor(prod_t[:, slot, :].rearrange("p (l b) -> p l b", b=P),
                                                turned[slot][:, :].rearrange("p (l b) -> p l b", b=P),
                                                item_t[:, :].unsqueeze(1).broadcast_to([P, G, P]), ALU.mult)\
                            .then_inc(product_ready, 1)

                    def add_item(g, slot):
                        dve.wait_ge(layer1_done, base + (g + 1))
                        columns = pre1[slot][0:A1, :].rearrange("p (l b) -> p l b", b=P)
                        nc.vector.tensor_tensor(columns, columns, item_part[:, :].unsqueeze(1).broadcast_to([A1, G, P]),
                                                ALU.add).then_inc(item_added, 1)

                    row_numbers(tile + 1, 1 - half)

                    nc.vector.tensor_copy(dense_now[:, :], dense_rows[:, tile, :]).then_inc(dense_ready, 1)
                    wait(dve, item_copied, tile + 1)
                    product(0, 0)
                    product(1, 1)
                    wait(dve, item_part_ready, tile + 1)
                    add_item(0, 0)
                    product(2, 0)
                    add_item(1, 1)
                    with dve.Fori(0, (EARLY - 3) // 2) as step:
                        for s in range(2):
                            g = step * 2 + (2 + s)
                            product(g + 1, 1 - s)
                            add_item(g, s)
                    add_item(EARLY - 1, 0)

                    def masked_logits(part, step_before):
                        nc.vector.tensor_scalar(logit[:, part], logits[:, part], bf[:, :], None, ALU.add).then_inc(softmax_step, 1)
                        wait(dve, softmax_step, step_before + 1)
                        nc.vector.copy_predicated(logit[:, part], masked[half][:, part], masked_logit[:, part])\
                            .then_inc(softmax_step, 1)
                        dve.wait_ge(softmax_step, step_before + 2)

                    before = tile * L

                    def add_group(g, begin=(None, None)):
                        for k in range(G):
                            row = hist[:, half, (g * G + k) * D:(g * G + k + 1) * D]
                            column = g * G + k // 2 + 2 * (k % 2)
                            by = weight[:, column:column + 1]
                            acc = odd_acc if k % 2 else even_acc
                            if k < 2 and begin[k] == "empty":
                                nc.vector.tensor_scalar(acc, row, by, None, ALU.mult).then_inc(sum_step, 1)
                            elif k < 2 and begin[k] == "early_sum":
                                nc.vector.scalar_tensor_tensor(acc, row, by, early_sum[:, :], ALU.mult, ALU.add)\
                                    .then_inc(sum_step, 1)
                            else:
                                dve.wait_ge(sum_step, before + (g * G + k - 1))
                                nc.vector.scalar_tensor_tensor(acc, row, by, acc, ALU.mult, ALU.add).then_inc(sum_step, 1)

                    early, late = slice(0, EARLY * G), slice(EARLY * G, L)
                    dve.wait_ge(early_logits_done, tile + 1)
                    masked_logits(early, tile * 4)
                    nc.vector.tensor_reduce(neg_max_early[:, :], logit[:, early], AX.X, ALU.max, negate=True)\
                        .then_inc(early_max_ready, 1)
                    product(EARLY, EARLY % 2)
                    wait(dve, early_weights_ready, tile + 1)
                    add_group(0, begin=("empty", "empty"))
                    add_group(1)
                    add_item(EARLY, EARLY % 2)
                    add_group(2)
                    add_group(3)
                    product(EARLY + 1, (EARLY + 1) % 2)
                    add_group(4)
                    add_group(5)
                    add_item(EARLY + 1, (EARLY + 1) % 2)
                    product(EARLY + 2, (EARLY + 2) % 2)
                    add_group(6)
                    dve.wait_ge(sum_step, before + EARLY * G)
                    nc.vector.tensor_copy(odd_sum[:, :], odd_acc).then_inc(early_sum_step, 1)
                    dve.wait_ge(early_sum_step, tile * 3 + 1)
                    nc.vector.tensor_tensor(early_sum[:, :], even_acc, odd_sum[:, :], ALU.add).then_inc(early_sum_step, 1)
                    add_item(EARLY + 2, (EARLY + 2) % 2)

                    dve.wait_ge(logits_done, tile + 1)
                    masked_logits(late, tile * 4 + 2)
                    nc.vector.tensor_reduce(neg_max_late[:, :], logit[:, late], AX.X, ALU.max, negate=True).then_inc(merge_step, 1)
                    dve.wait_ge(merge_step, tile * 2 + 1)
                    nc.vector.tensor_tensor(neg_max[:, :], neg_max_early[:, :], neg_max_late[:, :], ALU.min).then_inc(max_ready, 1)
                    wait(dve, weights_ready, tile + 1)
                    nc.vector.tensor_scalar(early_sum[:, :], early_sum[:, :], rescale[:, :], None, ALU.mult)\
                        .then_inc(early_sum_step, 1)
                    nc.vector.scalar_tensor_tensor(total[:, :], total_early[:, :], rescale[:, :], total_late[:, :],
                                                   ALU.mult, ALU.add).then_inc(merge_step, 1)
                    dve.wait_ge(early_sum_step, tile * 3 + 3)
                    add_group(EARLY, begin=("early_sum", "empty"))
                    dve.wait_ge(merge_step, tile * 2 + 2)
                    nc.vector.reciprocal(inv_total[:, :], total[:, :])
                    for g in range(EARLY + 1, GROUPS):
                        add_group(g)
                    dve.wait_ge(sum_step, before + L)
                    nc.vector.tensor_scalar(odd_sum[:, :], odd_acc, inv_total[:, :], None, ALU.mult).then_inc(user_step, 1)
                    dve.wait_ge(user_step, tile + 1)
                    nc.vector.scalar_tensor_tensor(user[:, :], even_acc, inv_total[:, :], odd_sum[:, :], ALU.mult, ALU.add)\
                        .then_inc(user_ready, 1)

                    dve.wait_ge(z1_ready, tile + 1)
                    nc.vector.tensor_scalar(n1[:, :], z1[:, :], 0.0, fa1[:, :], ALU.min, ALU.mult).then_inc(n1_ready, 1)
                    dve.wait_ge(n1_ready, tile + 1)
                    nc.vector.scalar_tensor_tensor(y1[:, :], z1[:, :], 0.0, n1[:, :], ALU.max, ALU.add).then_inc(y1_ready, 1)
                    dve.wait_ge(z2_ready, tile + 1)
                    nc.vector.tensor_scalar(n2[:, :], z2[:, :], 0.0, fa2[:, :], ALU.min, ALU.mult).then_inc(n2_ready, 1)
                    dve.wait_ge(n2_ready, tile + 1)
                    nc.vector.scalar_tensor_tensor(y2[:, :], z2[:, :], 0.0, n2[:, :], ALU.max, ALU.add).then_inc(y2_ready, 1)


INPUTS = ["r_dense_inputs", "r_sparse_inputs", "r_seq_inputs", "r_item_inputs", "L0_rec_emb_sparse", "L0_rec_emb_seq",
          "L0_rec_att_W1", "L0_rec_att_b1", "L0_rec_att_W2", "L0_rec_att_b2", "L0_rec_att_Wf", "L0_rec_att_bf",
          "L0_rec_bn_gamma", "L0_rec_bn_beta", "L0_rec_bn_mean", "L0_rec_bn_var", "L0_rec_ffn_W1", "L0_rec_ffn_b1",
          "L0_rec_ffn_a1", "L0_rec_ffn_W2", "L0_rec_ffn_b2", "L0_rec_ffn_a2", "L0_rec_out_W", "L0_rec_out_b"]


def kernel(**inputs):
    import numpy as _np
    import concourse.bacc as _bacc
    from concourse import mybir as _mybir
    from concourse.bass_utils import run_bass_kernel_spmd as _run

    nc = _bacc.Bacc("TRN2", target_bir_lowering=False, num_devices=1)
    arrays, args = {}, []
    for name in INPUTS:
        a = _np.ascontiguousarray(inputs[name])
        arrays[f"in_{name}_dram"] = a
        args.append(nc.dram_tensor(f"in_{name}_dram", a.shape, _mybir.dt.from_np(a.dtype), kind="ExternalInput").ap())
    arrays["identity_dram"] = _np.eye(128, dtype=_np.float32)
    args.append(nc.dram_tensor("identity_dram", (128, 128), _mybir.dt.float32, kind="ExternalInput").ap())
    rows = inputs["r_dense_inputs"].shape[0]
    args.append(nc.dram_tensor("out_0_dram", (rows, 1), _mybir.dt.float32, kind="ExternalOutput").ap())
    build(nc, *args)
    r = _run(nc, [arrays], core_ids=[0])
    return r.results[0]["out_0_dram"]
```

```python
from contextlib import ExitStack

import concourse.bass as bass
from concourse import mybir

F32 = mybir.dt.float32
I32 = mybir.dt.int32
ALU = mybir.AluOpType
ACT = mybir.ActivationFunctionType
AX = mybir.AxisListType

P = 128
MASKED = -2.0 ** 32 + 1
BN_EPS = 0.001


def build(nc, dense, sparse, seq, item, emb_sparse, emb_seq, att_w1, att_b1, att_w2, att_b2, att_wf, att_bf,
          bn_gamma, bn_beta, bn_mean, bn_var, ffn_w1, ffn_b1, ffn_a1, ffn_w2, ffn_b2, ffn_a2, out_w, out_b, identity, out):
    ROWS, L, NB = seq.shape
    V, E = emb_seq.shape[1:]
    NS, ND = sparse.shape[1], dense.shape[1]
    D = NB * E
    A1, A2 = att_w2.shape
    H1, H2 = ffn_w2.shape
    TILES = ROWS // P
    PAIRS = TILES // 2
    G = 4
    GROUPS = L // G
    N = G * P
    SEQ, NX = L * NB, L * NB + NB
    W = 2 * P
    EARLY = 7
    UP = 64
    assert D == P and A2 <= UP and TILES % 2 == 0 and GROUPS % 2 == 0 and EARLY == 7 and GROUPS == 10

    seq_table = emb_seq.rearrange("n v e -> (n v) e")
    sparse_table = emb_sparse.rearrange("n v e -> (n v) e")
    USER, ITEM, DENSE = (0, D), (D, D), (2 * D, ND)
    SPARSE_A, SPARSE_B = (2 * D + ND, 2 * E), (2 * D + ND + 2 * E, (NS - 2) * E)
    CHUNKS = [USER, ITEM, DENSE, SPARSE_A, SPARSE_B]

    ctx = ExitStack()
    with ctx:
        def sb(name, shape, dt=F32):
            return ctx.enter_context(nc.sbuf_tensor(name, shape, dt))

        def ps(name):
            return ctx.enter_context(nc.psum_tensor(name, [P, 512], F32))

        def sem(name):
            return ctx.enter_context(nc.semaphore(name))

        raw = sb("raw", [P, TILES + 1, NX], I32)
        raw_sparse = sb("raw_sparse", [P, TILES, NS], I32)
        wrap_sparse = sb("wrap_sparse", [P, TILES, NS])
        idx_sparse = sb("idx_sparse", [P, TILES, NS], I32)
        wrap = sb("wrap", [P, NX])
        table_start = sb("table_start", [P, NX])
        idx = [sb(f"idx{h}", [P, NX], I32) for h in range(2)]
        masked = [sb(f"masked{h}", [P, L], I32) for h in range(2)]
        masked_logit = sb("masked_logit", [P, L])
        hist = sb("hist", [P, 2, L * D])
        items = sb("items", [P, 2, D])
        sparse_rows = sb("sparse_rows", [P, TILES, NS * E])
        dense_rows = sb("dense_rows", [P, TILES, ND])
        dense_now = sb("dense_now", [P, ND])
        ident = sb("ident", [P, P])
        w1_raw = sb("w1_raw", [P, 4, A1])
        w1_item = sb("w1_item", [P, A1])
        w1_hist = sb("w1_hist", [P, A1])
        w1_prod = w1_raw[:, 3, :]
        b1 = sb("b1", [A1, 1])
        w2 = sb("w2", [A1, UP])
        b2 = sb("b2", [P, 1])
        wf = sb("wf", [P, 2])
        bf = sb("bf", [P, 1])
        fw1 = sb("fw1", [P, len(CHUNKS), H1])
        fb1 = sb("fb1", [H1, 1])
        fa1 = sb("fa1", [H1, 1])
        fw2 = sb("fw2", [H1, H2])
        fb2 = sb("fb2", [H2, 1])
        fa2 = sb("fa2", [H2, 1])
        ow = sb("ow", [H2, 1])
        ob = sb("ob", [1, 1])
        bn = sb("bn", [P, 4, len(CHUNKS)])
        bn_x = sb("bn_x", [P, 3, len(CHUNKS)])
        std = sb("std", [P, len(CHUNKS)])
        eps = sb("eps", [P, 1])
        bn_scale = sb("bn_scale", [P, len(CHUNKS)])
        bn_shift = sb("bn_shift", [P, len(CHUNKS)])
        hist_t = sb("hist_t", [P, 2, N])
        prod_t = sb("prod_t", [P, 2, N])
        hidden1 = sb("hidden1", [A1, 2, N])
        hidden2 = sb("hidden2", [P, N // 2])
        item_t = sb("item_t", [P, P])
        item_part = sb("item_part", [A1, P])
        logit = sb("logit", [P, L])
        neg_max_early = sb("neg_max_early", [P, 1])
        neg_max_late = sb("neg_max_late", [P, 1])
        neg_max = sb("neg_max", [P, 1])
        weight = sb("weight", [P, L])
        total_early = sb("total_early", [P, 1])
        total_late = sb("total_late", [P, 1])
        rescale = sb("rescale", [P, 1])
        total = sb("total", [P, 1])
        inv_total = sb("inv_total", [P, 1])
        early_sum = sb("early_sum", [P, D])
        odd_sum = sb("odd_sum", [P, D])
        user = sb("user", [P, D])
        x = sb("x", [P, 3, P])
        part = sb("part", [H1, ROWS])
        x_sparse = sb("x_sparse", [P, 2, W])
        z1 = sb("z1", [H1, W])
        n1 = sb("n1", [H1, W])
        y1 = sb("y1", [H1, W])
        z2 = sb("z2", [H2, W])
        n2 = sb("n2", [H2, W])
        y2 = sb("y2", [H2, W])
        score = sb("score", [1, ROWS])

        turned = [ps(f"turned{s}") for s in range(2)]
        pre1 = [ps(f"pre1{s}") for s in range(2)]
        pre2 = ps("pre2")
        logits = ps("logits")
        small = ps("small")
        sums = ps("sums")
        even_acc, odd_acc = sums[:, 0:D], sums[:, D:2 * D]

        idx_loaded = sem("idx_loaded")
        idx_rest_loaded = sem("idx_rest_loaded")
        att_weights_loaded = sem("att_weights_loaded")
        ffn_weights_loaded = sem("ffn_weights_loaded")
        stored = sem("stored")
        padded = sem("padded")
        dense_ready = sem("dense_ready")
        ident_ready = sem("ident_ready")
        w1_ready = sem("w1_ready")
        bn_step = sem("bn_step")
        bn_ready = sem("bn_ready")
        std_ready = sem("std_ready")
        idx_ready = sem("idx_ready")
        idx_step = sem("idx_step")
        items_landed = [sem(f"items_landed{h}") for h in range(2)]
        sparse_landed = [sem(f"sparse_landed{p}") for p in range(PAIRS)]
        group_landed = [sem(f"group_landed{s}") for s in range(2)]
        last_landed = [sem(f"last_landed{h}") for h in range(2)]
        group_ready = sem("group_ready")
        tile_consumed = sem("tile_consumed")
        group_turned = sem("group_turned")
        group_copied = sem("group_copied")
        product_ready = sem("product_ready")
        layer1_done = sem("layer1_done")
        item_added = sem("item_added")
        hidden1_ready = sem("hidden1_ready")
        layer2_done = sem("layer2_done")
        hidden2_ready = sem("hidden2_ready")
        item_turned = sem("item_turned")
        item_copied = sem("item_copied")
        item_part_done = sem("item_part_done")
        item_part_ready = sem("item_part_ready")
        logits_done = sem("logits_done")
        softmax_step = sem("softmax_step")
        early_logits_done = sem("early_logits_done")
        early_max_ready = sem("early_max_ready")
        early_weights_ready = sem("early_weights_ready")
        early_sum_step = sem("early_sum_step")
        max_ready = sem("max_ready")
        weights_ready = sem("weights_ready")
        merge_step = sem("merge_step")
        sum_step = sem("sum_step")
        user_step = sem("user_step")
        user_ready = sem("user_ready")
        sparse_idx_step = sem("sparse_idx_step")
        sparse_idx_ready = sem("sparse_idx_ready")
        sparse_turned = sem("sparse_turned")
        sparse_copied = sem("sparse_copied")
        part_done = sem("part_done")
        part_ready = sem("part_ready")
        user_turned = sem("user_turned")
        user_copied = sem("user_copied")
        ffn1_done = sem("ffn1_done")
        z1_step = sem("z1_step")
        y1_ready = sem("y1_ready")
        ffn2_done = sem("ffn2_done")
        z2_ready = sem("z2_ready")
        n2_ready = sem("n2_ready")
        y2_ready = sem("y2_ready")
        score_done = sem("score_done")
        score_ready = sem("score_ready")

        def wait(eng, semaphore, count):
            eng.wait_ge(semaphore, count)
            eng.nop(nofuse=True)

        block = ctx.enter_context(nc.Block())

        @block.sync
        def _(sp):
            seq_t = seq.rearrange("(t p) l n -> p t (l n)", p=P)
            item_tiles = item.rearrange("(t p) n -> p t n", p=P)
            sparse_tiles = sparse.rearrange("(t p) n -> p t n", p=P)
            with nc.allow_non_contiguous_dma(reason="short index rows and vectors by partition"):
                sp.dma_start(raw[:, 0, 0:SEQ], seq_t[:, 0, :]).then_inc(idx_loaded, 16)
                sp.dma_start(raw[:, 0, SEQ:NX], item_tiles[:, 0, :]).then_inc(idx_loaded, 16)
                sp.dma_start(ident[:, :], identity).then_inc(ident_ready, 16)
                sp.dma_start(w1_raw[:, :, :], att_w1.rearrange("(c p) n -> p c n", p=P)).then_inc(att_weights_loaded, 16)
                sp.dma_start(b1[:, :], att_b1.rearrange("(p o) -> p o", o=1)).then_inc(att_weights_loaded, 16)
                sp.wait_ge(padded, 1)
                sp.dma_start(w2[:, 0:A2], att_w2).then_inc(att_weights_loaded, 16)
                for half in range(2):
                    rows = slice(UP * half, UP * half + A2)
                    sp.dma_start(b2[rows, :], att_b2.rearrange("(p o) -> p o", o=1)).then_inc(att_weights_loaded, 16)
                    sp.dma_start(wf[rows, half:half + 1], att_wf).then_inc(att_weights_loaded, 16)
                sp.dma_start(bf[:, :], att_bf.rearrange("(p o) -> p o", o=1).broadcast_to([P, 1]))\
                    .then_inc(att_weights_loaded, 16)
                sp.dma_start(raw[:, 1:TILES, 0:SEQ], seq_t[:, 1:TILES, :]).then_inc(idx_rest_loaded, 16)
                sp.dma_start(raw[:, 1:TILES, SEQ:NX], item_tiles[:, 1:TILES, :]).then_inc(idx_rest_loaded, 16)
                sp.dma_start(raw_sparse[:, :, :], sparse_tiles).then_inc(idx_rest_loaded, 16)
                sp.dma_start(dense_rows[:, :, :], dense.rearrange("(t p) n -> p t n", p=P)).then_inc(ffn_weights_loaded, 16)
                for c, (first, k) in enumerate(CHUNKS):
                    sp.dma_start(fw1[0:k, c, :], ffn_w1[first:first + k, :]).then_inc(ffn_weights_loaded, 16)
                    for v, vector in enumerate((bn_gamma, bn_beta, bn_mean, bn_var)):
                        sp.dma_start(bn[0:k, v, c:c + 1], vector[first:first + k].rearrange("(p o) -> p o", o=1))\
                            .then_inc(ffn_weights_loaded, 16)
                for tile, vector in ((fb1, ffn_b1), (fa1, ffn_a1), (fb2, ffn_b2), (fa2, ffn_a2), (ob, out_b)):
                    sp.dma_start(tile[:, :], vector.rearrange("(p o) -> p o", o=1)).then_inc(ffn_weights_loaded, 16)
                sp.dma_start(fw2[:, :], ffn_w2).then_inc(ffn_weights_loaded, 16)
                sp.dma_start(ow[:, :], out_w).then_inc(ffn_weights_loaded, 16)
            sp.wait_ge(score_ready, PAIRS)
            sp.dma_start(out.rearrange("r o -> o r"), score[:, :]).then_inc(stored, 16)
            sp.wait_ge(stored, 16)

        ATT_LOADS = 16 * 8
        FFN_LOADS = 16 * (1 + 5 * len(CHUNKS) + 7)

        @block.gpsimd
        def _(gp):
            def gather(rows, table, index, landed):
                gp.indirect_dma_start(rows, None, table, bass.IndirectOffsetOnAxis(ap=index, axis=0)).then_inc(landed, 16)

            with gp.Fori(0, PAIRS) as pair:
                for half in range(2):
                    tile = pair * 2 + half
                    wait(gp, idx_ready, tile + 1)
                    wait(gp, tile_consumed, tile + 1)
                    for n in range(NB):
                        gather(items[:, half, n * E:(n + 1) * E], seq_table, idx[half][:, SEQ + n:SEQ + n + 1],
                               items_landed[half])
                    for g in range(GROUPS):
                        landed = last_landed[half] if g == GROUPS - 1 else group_landed[g % 2]
                        for k in range(G * NB):
                            if g > 0 and k == 6:
                                used = (GROUPS - (g - 1) % 2) // 2
                                gp.wait_ge(group_landed[(g - 1) % 2], 16 * G * NB * (tile * used + (g - 1) // 2 + 1))
                                gp.nop(nofuse=True).then_inc(group_ready, 1)
                            c = g * G * NB + k
                            gather(hist[:, half, c * E:(c + 1) * E], seq_table, idx[half][:, c:c + 1], landed)
            gp.wait_ge(sparse_idx_ready, 1)
            for tile in range(TILES):
                for n in range(NS):
                    gather(sparse_rows[:, tile, n * E:(n + 1) * E], sparse_table, idx_sparse[:, tile, n:n + 1],
                           sparse_landed[tile // 2])

        @block.tensor
        def _(pe):
            pe.sem_inc(tile_consumed, 2)
            pe.wait_ge(ident_ready, 16)
            pe.wait_ge(att_weights_loaded, ATT_LOADS)
            pe.wait_ge(w1_ready, 1)

            with pe.Fori(0, PAIRS) as pair:
                for half in range(2):
                    tile = pair * 2 + half
                    base = tile * GROUPS

                    def turn_group(g):
                        if g < GROUPS - 1:
                            pe.wait_ge(group_ready, tile * (GROUPS - 1) + (g + 1))
                        else:
                            pe.wait_ge(last_landed[half], 16 * G * NB * (pair + 1))
                        for j in range(G):
                            step = g * G + j
                            last = nc.tensor.transpose(turned[g % 2][:, j * P:(j + 1) * P],
                                                       hist[:, half, step * D:(step + 1) * D], ident[:, :])
                        last.then_inc(group_turned, 1)

                    def layer1(g):
                        pe.wait_ge(group_copied, base + (g + 1))
                        nc.tensor.matmul(pre1[g % 2][0:A1, :], w1_hist[:, :], hist_t[:, g % 2, :], start=True, stop=False)
                        pe.wait_ge(product_ready, base + (g + 1))
                        nc.tensor.matmul(pre1[g % 2][0:A1, :], w1_prod, prod_t[:, g % 2, :], start=False, stop=True)\
                            .then_inc(layer1_done, 1)

                    def layer2(g):
                        pe.wait_ge(hidden1_ready, base + (g + 1))
                        for k in range(2):
                            last = nc.tensor.matmul(pre2[UP * k:UP * (k + 1), 0:N // 2], w2[:, :],
                                                    hidden1[:, g % 2, k * N // 2:(k + 1) * N // 2], start=True, stop=True)
                        last.then_inc(layer2_done, 1)

                    def logits_of(g):
                        pe.wait_ge(hidden2_ready, base + (g + 1))
                        for j in range(2):
                            last = nc.tensor.matmul(logits[:, g * G + 2 * j:g * G + 2 * j + 2],
                                                    hidden2[:, j * P:(j + 1) * P], wf[:, :], start=True, stop=True)
                        return last

                    pe.wait_ge(items_landed[half], 16 * NB * (pair + 1))
                    nc.tensor.transpose(small[:, 0:P], items[:, half, :], ident[:, :])
                    pe.wait_ge(dense_ready, tile + 1)
                    nc.tensor.transpose(small[0:ND, 2 * P:3 * P], dense_now[:, :], ident[:, :]).then_inc(item_turned, 1)
                    pe.wait_ge(item_copied, tile + 1)
                    nc.tensor.matmul(small[0:A1, P:2 * P], w1_item[:, :], item_t[:, :], start=True, stop=True)\
                        .then_inc(item_part_done, 1)

                    turn_group(0)
                    for g in range(EARLY):
                        if g + 1 < EARLY:
                            turn_group(g + 1)
                        layer1(g)
                        if g >= 2:
                            logits_of(g - 2)
                        if g >= 1:
                            layer2(g - 1)
                    logits_of(EARLY - 2)
                    layer2(EARLY - 1)
                    logits_of(EARLY - 1).then_inc(early_logits_done, 1)
                    turn_group(EARLY)
                    layer1(EARLY)
                    layer2(EARLY)
                    logits_of(EARLY)
                    turn_group(EARLY + 1)
                    layer1(EARLY + 1)
                    turn_group(EARLY + 2)
                    layer1(EARLY + 2)
                    layer2(EARLY + 1)
                    logits_of(EARLY + 1)
                    layer2(EARLY + 2)
                    logits_of(EARLY + 2).then_inc(logits_done, 1)

                    pe.wait_ge(item_part_ready, tile + 1)
                    pe.wait_ge(user_ready, tile + 1)
                    nc.tensor.transpose(small[:, 3 * P:4 * P], user[:, :], ident[:, :]).then_inc(user_turned, 1)
                    for c in (1, 2, 0):
                        if c == 0:
                            pe.wait_ge(user_copied, tile + 1)
                            pe.sem_inc(tile_consumed, 1)
                        k = CHUNKS[c][1]
                        last = nc.tensor.matmul(logits[0:H1, P:2 * P], fw1[0:k, c, :], x[0:k, c, :], start=(c == 1),
                                                stop=(c == 0))
                    last.then_inc(part_done, 1)
                    pe.wait_ge(part_ready, tile + 1)

            def turn_sparse(p):
                pe.wait_ge(sparse_landed[p], 2 * 16 * NS)
                for h in range(2):
                    rows = sparse_rows[:, 2 * p + h, :]
                    nc.tensor.transpose(turned[0][:, h * P:(h + 1) * P], rows[:, 0:2 * E], ident[:, :])
                    last = nc.tensor.transpose(turned[0][0:SPARSE_B[1], W + h * P:W + (h + 1) * P], rows[:, 2 * E:NS * E],
                                               ident[:, :])
                last.then_inc(sparse_turned, 1)

            def ffn1(p):
                pe.wait_ge(sparse_copied, p + 1)
                nc.tensor.matmul(pre1[0][0:H1, 0:W], fw1[:, 3, :], x_sparse[:, 0, :], start=True, stop=False)
                nc.tensor.matmul(pre1[0][0:H1, 0:W], fw1[0:SPARSE_B[1], 4, :], x_sparse[0:SPARSE_B[1], 1, :], start=False,
                                 stop=True).then_inc(ffn1_done, 1)

            def ffn2(p):
                pe.wait_ge(y1_ready, p + 1)
                nc.tensor.matmul(pre2[0:H2, 0:W], fw2[:, :], y1[:, :], start=True, stop=True).then_inc(ffn2_done, 1)

            def output(p):
                pe.wait_ge(y2_ready, p + 1)
                if p > 0:
                    pe.wait_ge(score_ready, p)
                nc.tensor.matmul(logits[0:1, 0:W], ow[:, :], y2[:, :], start=True, stop=True).then_inc(score_done, 1)

            for p in range(PAIRS):
                turn_sparse(p)
                if p > 0:
                    ffn2(p - 1)
                ffn1(p)
                if p > 0:
                    output(p - 1)
            ffn2(PAIRS - 1)
            output(PAIRS - 1)

        @block.scalar
        def _(act):
            act.wait_ge(ffn_weights_loaded, FFN_LOADS)
            act.wait_ge(padded, 1)
            nc.scalar.activation(std[:, :], bn[:, 3, :], ACT.Sqrt, bias=eps[:, :]).then_inc(std_ready, 1)
            act.wait_ge(bn_ready, 1)

            def normalised(to, c, region):
                k = CHUNKS[c][1]
                return nc.scalar.activation(to, region, ACT.Identity, scale=bn_scale[0:k, c:c + 1],
                                            bias=bn_shift[0:k, c:c + 1])

            with act.Fori(0, PAIRS) as pair:
                for half in range(2):
                    tile = pair * 2 + half
                    base = tile * GROUPS

                    def copy_group(g, slot):
                        act.wait_ge(group_turned, base + (g + 1))
                        nc.scalar.copy(hist_t[:, slot, :], turned[slot][:, :]).then_inc(group_copied, 1)

                    def sigmoid1(g, slot):
                        act.wait_ge(item_added, base + (g + 1))
                        nc.scalar.activation(hidden1[:, slot, :], pre1[slot][0:A1, :], ACT.Sigmoid).then_inc(hidden1_ready, 1)

                    def sigmoid2(g):
                        act.wait_ge(layer2_done, base + (g + 1))
                        nc.scalar.activation(hidden2[:, :], pre2[:, 0:N // 2], ACT.Sigmoid, bias=b2[:, :])\
                            .then_inc(hidden2_ready, 1)

                    act.wait_ge(item_turned, tile + 1)
                    normalised(x[:, 1, :], 1, small[:, 0:P])
                    normalised(x[0:ND, 2, :], 2, small[0:ND, 2 * P:3 * P])
                    nc.scalar.copy(item_t[:, :], small[:, 0:P]).then_inc(item_copied, 1)
                    act.wait_ge(item_part_done, tile + 1)
                    nc.scalar.activation(item_part[:, :], small[0:A1, P:2 * P], ACT.Identity, bias=b1[:, :])\
                        .then_inc(item_part_ready, 1)

                    copy_group(0, 0)
                    copy_group(1, 1)
                    sigmoid1(0, 0)
                    copy_group(2, 0)
                    sigmoid1(1, 1)
                    with act.Fori(0, (EARLY - 3) // 2) as step:
                        for s in range(2):
                            g = step * 2 + (2 + s)
                            sigmoid2(g - 2)
                            copy_group(g + 1, 1 - s)
                            sigmoid1(g, s)
                    sigmoid2(EARLY - 3)
                    sigmoid1(EARLY - 1, 0)
                    sigmoid2(EARLY - 2)
                    sigmoid2(EARLY - 1)
                    copy_group(EARLY, EARLY % 2)
                    act.preload_act_table(ACT.Exp)
                    act.wait_ge(early_max_ready, tile + 1)
                    nc.scalar.activation(weight[:, 0:EARLY * G], logit[:, 0:EARLY * G], ACT.Exp, bias=neg_max_early[:, :],
                                         accum_out=total_early[:, :]).then_inc(early_weights_ready, 1)
                    act.preload_act_table(ACT.Sigmoid)
                    sigmoid1(EARLY, 1)
                    sigmoid2(EARLY)
                    copy_group(EARLY + 1, 0)
                    sigmoid1(EARLY + 1, 0)
                    copy_group(EARLY + 2, 1)
                    sigmoid2(EARLY + 1)
                    sigmoid1(EARLY + 2, 1)
                    sigmoid2(EARLY + 2)

                    act.preload_act_table(ACT.Exp)
                    act.wait_ge(max_ready, tile + 1)
                    nc.scalar.activation(rescale[:, :], neg_max_early[:, :], ACT.Exp, bias=neg_max[:, :], scale=-1.0)
                    nc.scalar.activation(weight[:, EARLY * G:L], logit[:, EARLY * G:L], ACT.Exp, bias=neg_max[:, :],
                                         accum_out=total_late[:, :]).then_inc(weights_ready, 1)
                    act.preload_act_table(ACT.Sigmoid)
                    act.wait_ge(user_turned, tile + 1)
                    normalised(x[:, 0, :], 0, small[:, 3 * P:4 * P]).then_inc(user_copied, 1)
                    wait(act, part_done, tile + 1)
                    nc.scalar.activation(part[:, bass.ds(tile * P, P)], logits[0:H1, P:2 * P], ACT.Identity, bias=fb1[:, :])\
                        .then_inc(part_ready, 1)

            def copy_sparse(p):
                act.wait_ge(sparse_turned, p + 1)
                k = SPARSE_B[1]
                normalised(x_sparse[:, 0, :], 3, turned[0][:, 0:W])
                normalised(x_sparse[0:k, 1, :], 4, turned[0][0:k, W:2 * W]).then_inc(sparse_copied, 1)

            def add_bias2(p):
                act.wait_ge(ffn2_done, p + 1)
                nc.scalar.activation(z2[:, :], pre2[0:H2, 0:W], ACT.Identity, bias=fb2[:, :]).then_inc(z2_ready, 1)

            def score_of(p):
                wait(act, score_done, p + 1)
                nc.scalar.activation(score[:, bass.ds(p * W, W)], logits[0:1, 0:W], ACT.Sigmoid, bias=ob[:, :])\
                    .then_inc(score_ready, 1)

            copy_sparse(0)
            with act.Fori(1, PAIRS) as p:
                copy_sparse(p)
                add_bias2(p - 1)
                score_of(p - 1)
            add_bias2(PAIRS - 1)
            score_of(PAIRS - 1)

        @block.vector
        def _(dve):
            nc.vector.memset(w2[:, :], 0.0)
            nc.vector.memset(b2[:, :], 0.0)
            nc.vector.memset(wf[:, :], 0.0)
            nc.vector.memset(bn[:, :, :], 1.0)
            nc.vector.memset(raw[:, TILES, :], 0)
            nc.vector.memset(masked_logit[:, :], MASKED)
            nc.vector.memset(eps[:, :], BN_EPS)
            for n in range(NB):
                last = nc.vector.memset(table_start[:, n:NX:NB], float(n * V))
            last.then_inc(padded, 1)
            dve.wait_ge(padded, 1)

            def row_numbers(tile, half):
                before = tile * 3
                nc.vector.tensor_scalar(wrap[:, :], raw[:, tile, :], 0.0, float(V), ALU.is_lt, ALU.mult).then_inc(idx_step, 1)
                dve.wait_ge(idx_step, before + 1)
                nc.vector.tensor_tensor(wrap[:, :], wrap[:, :], raw[:, tile, :], ALU.add).then_inc(idx_step, 1)
                dve.wait_ge(idx_step, before + 2)
                nc.vector.tensor_scalar(wrap[:, :], wrap[:, :], 0.0, float(V - 1), ALU.max, ALU.min).then_inc(idx_step, 1)
                dve.wait_ge(idx_step, before + 3)
                nc.vector.tensor_tensor(idx[half][:, :], wrap[:, :], table_start[:, :], ALU.add).then_inc(idx_ready, 1)
                nc.vector.tensor_scalar(masked[half][:, :].rearrange("p (g j k) -> p g j k", j=2, k=2),
                                        raw[:, tile, 0:SEQ:NB].rearrange("p (g k j) -> p g j k", k=2, j=2),
                                        0.0, None, ALU.is_equal)

            dve.wait_ge(idx_loaded, 32)
            row_numbers(0, 0)

            dve.wait_ge(att_weights_loaded, ATT_LOADS)
            nc.vector.tensor_tensor(w1_item[:, :], w1_raw[:, 0, :], w1_raw[:, 2, :], ALU.add)
            nc.vector.tensor_tensor(w1_hist[:, :], w1_raw[:, 1, :], w1_raw[:, 2, :], ALU.subtract).then_inc(w1_ready, 1)

            v, r, t = (bn_x[:, i, :] for i in range(3))
            steps = [0]

            def settled(instruction):
                steps[0] += 1
                instruction.then_inc(bn_step, 1)
                dve.wait_ge(bn_step, steps[0])

            dve.wait_ge(ffn_weights_loaded, FFN_LOADS)
            settled(nc.vector.tensor_scalar(v, bn[:, 3, :], BN_EPS, None, ALU.add))
            dve.wait_ge(std_ready, 1)
            settled(nc.vector.reciprocal(r, std[:, :]))
            settled(nc.vector.tensor_tensor(t, r, r, ALU.mult))
            settled(nc.vector.tensor_tensor(t, t, v, ALU.mult))
            settled(nc.vector.tensor_scalar(t, t, -0.5, 1.5, ALU.mult, ALU.add))
            settled(nc.vector.tensor_tensor(r, r, t, ALU.mult))
            settled(nc.vector.tensor_tensor(bn_scale[:, :], bn[:, 0, :], r, ALU.mult))
            settled(nc.vector.tensor_tensor(t, bn[:, 2, :], bn_scale[:, :], ALU.mult))
            nc.vector.tensor_tensor(bn_shift[:, :], bn[:, 1, :], t, ALU.subtract).then_inc(bn_ready, 1)

            dve.wait_ge(idx_rest_loaded, 48)
            nc.vector.tensor_scalar(wrap_sparse[:, :, :], raw_sparse[:, :, :], 0.0, float(V), ALU.is_lt, ALU.mult)\
                .then_inc(sparse_idx_step, 1)
            dve.wait_ge(sparse_idx_step, 1)
            nc.vector.tensor_tensor(wrap_sparse[:, :, :], wrap_sparse[:, :, :], raw_sparse[:, :, :], ALU.add)\
                .then_inc(sparse_idx_step, 1)
            dve.wait_ge(sparse_idx_step, 2)
            nc.vector.tensor_scalar(wrap_sparse[:, :, :], wrap_sparse[:, :, :], 0.0, float(V - 1), ALU.max, ALU.min)\
                .then_inc(sparse_idx_step, 1)
            dve.wait_ge(sparse_idx_step, 3)
            for n in range(NS):
                last = nc.vector.tensor_scalar(idx_sparse[:, :, n], wrap_sparse[:, :, n], float(n * V), None, ALU.add)
            last.then_inc(sparse_idx_ready, 1)

            with dve.Fori(0, PAIRS) as pair:
                for half in range(2):
                    tile = pair * 2 + half
                    base = tile * GROUPS

                    def product(g, slot):
                        dve.wait_ge(group_copied, base + (g + 1))
                        nc.vector.tensor_tensor(prod_t[:, slot, :].rearrange("p (l b) -> p l b", b=P),
                                                turned[slot][:, :].rearrange("p (l b) -> p l b", b=P),
                                                item_t[:, :].unsqueeze(1).broadcast_to([P, G, P]), ALU.mult)\
                            .then_inc(product_ready, 1)

                    def add_item(g, slot):
                        dve.wait_ge(layer1_done, base + (g + 1))
                        columns = pre1[slot][0:A1, :].rearrange("p (l b) -> p l b", b=P)
                        nc.vector.tensor_tensor(columns, columns, item_part[:, :].unsqueeze(1).broadcast_to([A1, G, P]),
                                                ALU.add).then_inc(item_added, 1)

                    row_numbers(tile + 1, 1 - half)

                    nc.vector.tensor_copy(dense_now[:, :], dense_rows[:, tile, :]).then_inc(dense_ready, 1)
                    wait(dve, item_copied, tile + 1)
                    product(0, 0)
                    product(1, 1)
                    wait(dve, item_part_ready, tile + 1)
                    add_item(0, 0)
                    product(2, 0)
                    add_item(1, 1)
                    with dve.Fori(0, (EARLY - 3) // 2) as step:
                        for s in range(2):
                            g = step * 2 + (2 + s)
                            product(g + 1, 1 - s)
                            add_item(g, s)
                    add_item(EARLY - 1, 0)

                    def masked_logits(part, step_before):
                        nc.vector.tensor_scalar(logit[:, part], logits[:, part], bf[:, :], None, ALU.add).then_inc(softmax_step, 1)
                        wait(dve, softmax_step, step_before + 1)
                        nc.vector.copy_predicated(logit[:, part], masked[half][:, part], masked_logit[:, part])\
                            .then_inc(softmax_step, 1)
                        dve.wait_ge(softmax_step, step_before + 2)

                    before = tile * L

                    def add_group(g, begin=(None, None)):
                        for k in range(G):
                            row = hist[:, half, (g * G + k) * D:(g * G + k + 1) * D]
                            column = g * G + k // 2 + 2 * (k % 2)
                            by = weight[:, column:column + 1]
                            acc = odd_acc if k % 2 else even_acc
                            if k < 2 and begin[k] == "empty":
                                nc.vector.tensor_scalar(acc, row, by, None, ALU.mult).then_inc(sum_step, 1)
                            elif k < 2 and begin[k] == "early_sum":
                                nc.vector.scalar_tensor_tensor(acc, row, by, early_sum[:, :], ALU.mult, ALU.add)\
                                    .then_inc(sum_step, 1)
                            else:
                                dve.wait_ge(sum_step, before + (g * G + k - 1))
                                nc.vector.scalar_tensor_tensor(acc, row, by, acc, ALU.mult, ALU.add).then_inc(sum_step, 1)

                    early, late = slice(0, EARLY * G), slice(EARLY * G, L)
                    dve.wait_ge(early_logits_done, tile + 1)
                    masked_logits(early, tile * 4)
                    nc.vector.tensor_reduce(neg_max_early[:, :], logit[:, early], AX.X, ALU.max, negate=True)\
                        .then_inc(early_max_ready, 1)
                    product(EARLY, EARLY % 2)
                    wait(dve, early_weights_ready, tile + 1)
                    add_group(0, begin=("empty", "empty"))
                    add_group(1)
                    add_item(EARLY, EARLY % 2)
                    add_group(2)
                    add_group(3)
                    product(EARLY + 1, (EARLY + 1) % 2)
                    add_group(4)
                    add_group(5)
                    add_item(EARLY + 1, (EARLY + 1) % 2)
                    product(EARLY + 2, (EARLY + 2) % 2)
                    add_group(6)
                    dve.wait_ge(sum_step, before + EARLY * G)
                    nc.vector.tensor_copy(odd_sum[:, :], odd_acc).then_inc(early_sum_step, 1)
                    dve.wait_ge(early_sum_step, tile * 3 + 1)
                    nc.vector.tensor_tensor(early_sum[:, :], even_acc, odd_sum[:, :], ALU.add).then_inc(early_sum_step, 1)
                    add_item(EARLY + 2, (EARLY + 2) % 2)

                    dve.wait_ge(logits_done, tile + 1)
                    masked_logits(late, tile * 4 + 2)
                    nc.vector.tensor_reduce(neg_max_late[:, :], logit[:, late], AX.X, ALU.max, negate=True).then_inc(merge_step, 1)
                    dve.wait_ge(merge_step, tile * 2 + 1)
                    nc.vector.tensor_tensor(neg_max[:, :], neg_max_early[:, :], neg_max_late[:, :], ALU.min).then_inc(max_ready, 1)
                    wait(dve, weights_ready, tile + 1)
                    nc.vector.tensor_scalar(early_sum[:, :], early_sum[:, :], rescale[:, :], None, ALU.mult)\
                        .then_inc(early_sum_step, 1)
                    nc.vector.scalar_tensor_tensor(total[:, :], total_early[:, :], rescale[:, :], total_late[:, :],
                                                   ALU.mult, ALU.add).then_inc(merge_step, 1)
                    dve.wait_ge(early_sum_step, tile * 3 + 3)
                    add_group(EARLY, begin=("early_sum", "empty"))
                    dve.wait_ge(merge_step, tile * 2 + 2)
                    nc.vector.reciprocal(inv_total[:, :], total[:, :])
                    for g in range(EARLY + 1, GROUPS):
                        add_group(g)
                    dve.wait_ge(sum_step, before + L)
                    nc.vector.tensor_scalar(odd_sum[:, :], odd_acc, inv_total[:, :], None, ALU.mult).then_inc(user_step, 1)
                    dve.wait_ge(user_step, tile + 1)
                    nc.vector.scalar_tensor_tensor(user[:, :], even_acc, inv_total[:, :], odd_sum[:, :], ALU.mult, ALU.add)\
                        .then_inc(user_ready, 1)

            def prelu1(p):
                dve.wait_ge(ffn1_done, p + 1)
                nc.vector.tensor_tensor(z1[:, :], pre1[0][0:H1, 0:W], part[:, bass.ds(p * W, W)], ALU.add).then_inc(z1_step, 1)
                dve.wait_ge(z1_step, 2 * p + 1)
                nc.vector.tensor_scalar(n1[:, :], z1[:, :], 0.0, fa1[:, :], ALU.min, ALU.mult).then_inc(z1_step, 1)
                dve.wait_ge(z1_step, 2 * p + 2)
                nc.vector.scalar_tensor_tensor(y1[:, :], z1[:, :], 0.0, n1[:, :], ALU.max, ALU.add).then_inc(y1_ready, 1)

            def prelu2(p):
                dve.wait_ge(z2_ready, p + 1)
                nc.vector.tensor_scalar(n2[:, :], z2[:, :], 0.0, fa2[:, :], ALU.min, ALU.mult).then_inc(n2_ready, 1)
                dve.wait_ge(n2_ready, p + 1)
                nc.vector.scalar_tensor_tensor(y2[:, :], z2[:, :], 0.0, n2[:, :], ALU.max, ALU.add).then_inc(y2_ready, 1)

            dve.wait_ge(part_ready, TILES)
            prelu1(0)
            with dve.Fori(1, PAIRS) as p:
                prelu2(p - 1)
                prelu1(p)
            prelu2(PAIRS - 1)


INPUTS = ["r_dense_inputs", "r_sparse_inputs", "r_seq_inputs", "r_item_inputs", "L0_rec_emb_sparse", "L0_rec_emb_seq",
          "L0_rec_att_W1", "L0_rec_att_b1", "L0_rec_att_W2", "L0_rec_att_b2", "L0_rec_att_Wf", "L0_rec_att_bf",
          "L0_rec_bn_gamma", "L0_rec_bn_beta", "L0_rec_bn_mean", "L0_rec_bn_var", "L0_rec_ffn_W1", "L0_rec_ffn_b1",
          "L0_rec_ffn_a1", "L0_rec_ffn_W2", "L0_rec_ffn_b2", "L0_rec_ffn_a2", "L0_rec_out_W", "L0_rec_out_b"]


def kernel(**inputs):
    import numpy as _np
    import concourse.bacc as _bacc
    from concourse import mybir as _mybir
    from concourse.bass_utils import run_bass_kernel_spmd as _run

    nc = _bacc.Bacc("TRN2", target_bir_lowering=False, num_devices=1)
    arrays, args = {}, []
    for name in INPUTS:
        a = _np.ascontiguousarray(inputs[name])
        arrays[f"in_{name}_dram"] = a
        args.append(nc.dram_tensor(f"in_{name}_dram", a.shape, _mybir.dt.from_np(a.dtype), kind="ExternalInput").ap())
    arrays["identity_dram"] = _np.eye(128, dtype=_np.float32)
    args.append(nc.dram_tensor("identity_dram", (128, 128), _mybir.dt.float32, kind="ExternalInput").ap())
    rows = inputs["r_dense_inputs"].shape[0]
    args.append(nc.dram_tensor("out_0_dram", (rows, 1), _mybir.dt.float32, kind="ExternalOutput").ap())
    build(nc, *args)
    r = _run(nc, [arrays], core_ids=[0])
    return r.results[0]["out_0_dram"]
```
